# Optimizing a Trainium2 kernel written in Bass

```python
import numpy as np
import jax
import jax.numpy as jnp

def _softmax(x, axis=-1):
    return jax.nn.softmax(x, axis=axis)

def _gelu(x):
    return jax.nn.gelu(x, approximate=True)

def _silu(x):
    return jax.nn.silu(x)

def _sigmoid(x):
    return jax.nn.sigmoid(x)

def _layernorm(x, axis=-1, eps=1e-05):
    m = jnp.mean(x, axis=axis, keepdims=True)
    v = jnp.var(x, axis=axis, keepdims=True)
    return (x - m) / jnp.sqrt(v + eps)

def _scatter_add(tgt, idx, src, axis=0):
    return tgt.at[idx].add(src)

def _segment_sum(src, seg, n):
    return jax.ops.segment_sum(src, seg, n)
kernel_name = 'mk_seq_preln_d1_jaxref_r8_18b121'

def setup_inputs(seed: int=0):
    np.random.seed(seed)
    _w = jnp.asarray

    def _L0_attn_setup():
        import jax, jax.numpy as jnp
        import numpy as np
        NUM_HEADS = 16
        D_MODEL = 128
        D_K = D_MODEL // NUM_HEADS
        MAX_SEQ_LEN = 512
        ROPE_BASE = 10000.0
        BATCH = 2
        SEQ_LEN = 256

        def _rope_tables(seq_len, d_k, base=ROPE_BASE):
            theta = 1.0 / base ** (jnp.arange(0, d_k, 2, dtype=jnp.float32) / d_k)
            m = jnp.arange(seq_len, dtype=jnp.float32)
            m_theta = jnp.outer(m, theta)
            ang = jnp.concatenate([m_theta, m_theta], axis=-1)
            return (jnp.cos(ang), jnp.sin(ang))

        def _apply_rope(x, cos, sin):
            d2 = x.shape[-1] // 2
            x1, x2 = (x[..., :d2], x[..., d2:])
            x_flip = jnp.concatenate([-x2, x1], axis=-1)
            return x * cos + x_flip * sin
        key = jax.random.key(seed)
        kx, kq, kk, kv, ko = jax.random.split(key, 5)
        s = 1.0 / np.sqrt(D_MODEL)
        x = jax.random.normal(kx, (BATCH, SEQ_LEN, D_MODEL), dtype=jnp.float32)
        W_Q = jax.random.uniform(kq, (D_MODEL, D_MODEL), jnp.float32, -s, s)
        W_K = jax.random.uniform(kk, (D_MODEL, D_MODEL), jnp.float32, -s, s)
        W_V = jax.random.uniform(kv, (D_MODEL, D_MODEL), jnp.float32, -s, s)
        W_O = jax.random.uniform(ko, (D_MODEL, D_MODEL), jnp.float32, -s, s)
        return {'x': x, 'W_Q': W_Q, 'W_K': W_K, 'W_V': W_V, 'W_O': W_O}
    _L0_attn_in = _L0_attn_setup()

    def _L0_ffn_setup():
        import jax, jax.numpy as jnp
        import numpy as np
        TOPK = 4
        key = jax.random.key(seed)
        ks = jax.random.split(key, 9)
        B, T, D = (4, 256, 128)
        E, H = (32, 128)
        HS = H * TOPK
        s = lambda k, shape, fan: jax.random.normal(k, shape, dtype=jnp.float32) / np.sqrt(fan)
        return {'x': jax.random.normal(ks[0], (B, T, D), dtype=jnp.float32), 'router_w': s(ks[1], (E, D), D), 'router_bias': jnp.zeros((E,), dtype=jnp.float32), 'gate_w': s(ks[2], (E, H, D), D), 'up_w': s(ks[3], (E, H, D), D), 'down_w': s(ks[4], (E, D, H), H), 'sgate_w': s(ks[5], (HS, D), D), 'sup_w': s(ks[6], (HS, D), D), 'sdown_w': s(ks[7], (D, HS), HS)}
    _L0_ffn_in = _L0_ffn_setup()
    _d = {'L0_attn_x': _L0_attn_in['x'], 'L0_attn_W_Q': _L0_attn_in['W_Q'], 'L0_attn_W_K': _L0_attn_in['W_K'], 'L0_attn_W_V': _L0_attn_in['W_V'], 'L0_attn_W_O': _L0_attn_in['W_O'], 'L0_ffn_router_w': _L0_ffn_in['router_w'], 'L0_ffn_router_bias': _L0_ffn_in['router_bias'], 'L0_ffn_gate_w': _L0_ffn_in['gate_w'], 'L0_ffn_up_w': _L0_ffn_in['up_w'], 'L0_ffn_down_w': _L0_ffn_in['down_w'], 'L0_ffn_sgate_w': _L0_ffn_in['sgate_w'], 'L0_ffn_sup_w': _L0_ffn_in['sup_w'], 'L0_ffn_sdown_w': _L0_ffn_in['sdown_w']}
    _x0 = _d['L0_attn_x']
    _d['L0_attn_x'] = jax.random.normal(jax.random.fold_in(jax.random.key(seed), 1), (1, 2048, 128), dtype=_x0.dtype)
    del _x0
    return _d

def reference(L0_attn_x, L0_attn_W_Q, L0_attn_W_K, L0_attn_W_V, L0_attn_W_O, L0_ffn_router_w, L0_ffn_router_bias, L0_ffn_gate_w, L0_ffn_up_w, L0_ffn_down_w, L0_ffn_sgate_w, L0_ffn_sup_w, L0_ffn_sdown_w):

    def _L0_attn_ref(x, W_Q, W_K, W_V, W_O):
        import jax, jax.numpy as jnp
        import numpy as np
        NUM_HEADS = 16
        D_MODEL = 128
        D_K = D_MODEL // NUM_HEADS
        MAX_SEQ_LEN = 512
        ROPE_BASE = 10000.0
        BATCH = 2
        SEQ_LEN = 256

        def _rope_tables(seq_len, d_k, base=ROPE_BASE):
            theta = 1.0 / base ** (jnp.arange(0, d_k, 2, dtype=jnp.float32) / d_k)
            m = jnp.arange(seq_len, dtype=jnp.float32)
            m_theta = jnp.outer(m, theta)
            ang = jnp.concatenate([m_theta, m_theta], axis=-1)
            return (jnp.cos(ang), jnp.sin(ang))

        def _apply_rope(x, cos, sin):
            d2 = x.shape[-1] // 2
            x1, x2 = (x[..., :d2], x[..., d2:])
            x_flip = jnp.concatenate([-x2, x1], axis=-1)
            return x * cos + x_flip * sin
        B, S, _ = x.shape

        def proj(W):
            y = jnp.einsum('bsd,ed->bse', x, W)
            return y.reshape(B, S, NUM_HEADS, D_K).transpose(0, 2, 1, 3)
        Q, K, V = (proj(W_Q), proj(W_K), proj(W_V))
        cos, sin = _rope_tables(S, D_K)
        Q = _apply_rope(Q, cos, sin)
        K = _apply_rope(K, cos, sin)
        scores = jnp.einsum('bhsd,bhtd->bhst', Q, K) / jnp.sqrt(jnp.float32(D_K))
        causal = jnp.tril(jnp.ones((S, S), dtype=bool))
        scores = jnp.where(causal[None, None], scores, -jnp.inf)
        attn = jax.nn.softmax(scores, axis=-1)
        out = jnp.einsum('bhst,bhtd->bhsd', attn, V)
        out = out.transpose(0, 2, 1, 3).reshape(B, S, D_MODEL)
        return jnp.einsum('bsd,ed->bse', out, W_O)

    def _L0_ffn_ref(x, router_w, router_bias, gate_w, up_w, down_w, sgate_w, sup_w, sdown_w):
        import jax, jax.numpy as jnp
        import numpy as np
        TOPK = 4
        B, T, D = x.shape
        flat = x.reshape(B * T, D)
        logits = flat.astype(jnp.float32) @ router_w.T + router_bias
        scores = jax.nn.softmax(logits, axis=-1)
        topk_scores, topk_idx = jax.lax.top_k(scores, TOPK)
        topk_scores = topk_scores / jnp.clip(topk_scores.sum(axis=-1, keepdims=True), 1e-12, None)
        h = jax.nn.silu(jnp.einsum('nd,ehd->neh', flat, gate_w)) * jnp.einsum('nd,ehd->neh', flat, up_w)
        expert_out = jnp.einsum('neh,edh->ned', h, down_w)
        sel = jnp.take_along_axis(expert_out, topk_idx[:, :, None], axis=1)
        out = (sel * topk_scores.astype(flat.dtype)[:, :, None]).sum(axis=1)
        out = out + jax.nn.silu(flat @ sgate_w.T) * (flat @ sup_w.T) @ sdown_w.T
        return out.reshape(B, T, D)
    x = L0_attn_x
    x = x + _L0_attn_ref(_layernorm(x, axis=-1), L0_attn_W_Q, L0_attn_W_K, L0_attn_W_V, L0_attn_W_O)
    x = x + _L0_ffn_ref(_layernorm(x, axis=-1), L0_ffn_router_w, L0_ffn_router_bias, L0_ffn_gate_w, L0_ffn_up_w, L0_ffn_down_w, L0_ffn_sgate_w, L0_ffn_sup_w, L0_ffn_sdown_w)
    return x

_drawn_inputs = setup_inputs


def setup_inputs(seed=0):
    import zlib

    import numpy as np

    out = dict(_drawn_inputs(seed))
    spreads = {'L0_ffn_router_bias': (0.0, 0.1)}
    factors = {'L0_attn_W_Q': 2.961, 'L0_attn_W_K': 2.758}
    for name, (base, spread) in spreads.items():
        noise = np.random.default_rng([zlib.crc32(name.encode()), seed]).standard_normal(out[name].shape)
        drawn = base * np.exp(spread * noise) if base else spread * noise
        out[name] = jnp.asarray(drawn.astype(out[name].dtype))
    for name, factor in factors.items():
        out[name] = (out[name] * factor).astype(out[name].dtype)
    return out
```

```python
from contextlib import ExitStack

import numpy as np

import concourse.bass as bass
from concourse import mybir

ALU = mybir.AluOpType
ACT = mybir.ActivationFunctionType
AX = mybir.AxisListType.X
F32 = mybir.dt.float32
F32R = mybir.dt.float32r
BF16 = mybir.dt.bfloat16
U32 = mybir.dt.uint32

P = 128
S = 2048
D = 128
NH = 16
DK = D // NH
HG = 4
NG = NH // HG
NT = S // P
BT = 512
NJ = S // BT
TJ = BT // P
NE = 32
TOPK = 4
NSH = 4
NX = NE + NSH
PIECES = 3
REPS = PIECES
ROWS = PIECES * REPS * DK
MROW = ROWS
SCALE = float(1.0 / np.sqrt(np.float32(DK)))
BIG = 1.0e30
EPS = 1e-5

STEPS = [(J, t) for J in range(NJ) for t in range(TJ * (J + 1))]
MAXES = [(J, i, c) for J in range(NJ) for i in range(TJ) for c in range(J + 1)]
NSTEP = len(STEPS)
LEAD = 21
ENDS = [TJ * (J + 1) * (J + 2) // 2 for J in range(NJ)]


def mixer(nc, x_in, wq_in, wk_in, wv_in, wo_in, rw_in, rb_in, gw_in, uw_in, dw_in, sg_in, su_in, sd_in,
          cos_in, sin_in, out):
    with ExitStack() as ctx:
        def sb(name, shape, dt, to=ctx):
            return to.enter_context(nc.sbuf_tensor(name, shape, dt))

        def sem(name):
            return ctx.enter_context(nc.semaphore(name))

        qp_d = nc.dram_tensor("qp_d", [NJ, PIECES, P, BT], BF16).ap()
        kp_d = nc.dram_tensor("kp_d", [NJ, 2 * PIECES - 1, P, BT], BF16).ap()
        zero_d = nc.dram_tensor("zero_d", [PIECES, HG * S], BF16).ap()
        wt_d = nc.dram_tensor("wt_d", [NX, S], F32).ap()

        xs = sb("xs", [P, NT, D], F32)
        xn = sb("xn", [P, NT, D], F32)
        xnT = sb("xnT", [P, S], F32)
        attn = sb("attn", [P, NT, D], F32)
        ident = sb("ident", [P, P], F32)
        negI = sb("negI", [P, P], BF16)
        later_k = sb("later_k", [P, P], BF16)
        later_p = sb("later_p", [P, P], BF16)
        iota_e = sb("iota_e", [P, NE], F32)
        iota_i = sb("iota_i", [P, NE], mybir.dt.int32)
        half = sb("half", [NSH, S], F32)
        stats = sb("stats", [P, NT, 6], F32)
        mv = sb("mv", [P, NT, 2], F32)
        std = sb("std", [P, NT], F32)
        rstd = sb("rstd", [P, NT], F32)
        eps = sb("eps", [P, 1], F32)
        wnat = sb("wnat", [P, 4, D], F32)
        wT = sb("wT", [P, 6, D], F32)
        rwn = sb("rwn", [NE, D], F32)
        rwT = sb("rwT", [P, NE], F32)
        bias = sb("bias", [P, NE], F32)

        attn_mem = ExitStack()
        qst = sb("qst", [P, 2, NJ, HG, BT], BF16, attn_mem)
        kst = sb("kst", [P, 2, NJ, HG, BT], BF16, attn_mem)
        vext = sb("vext", [P, NT, NH, DK + 1], F32, attn_mem)
        vcur = sb("vcur", [P, NT, HG, 32], F32, attn_mem)
        pmax = sb("pmax", [P, HG, TJ, NJ], F32, attn_mem)
        negm = sb("negm", [P, HG * TJ], F32, attn_mem)
        mres = sb("mres", [HG * TJ, 2, P], F32, attn_mem)
        mp = sb("mp", [HG * TJ, PIECES, P], BF16, attn_mem)
        ot = sb("ot", [P, BT], F32, attn_mem)
        rsum = sb("rsum", [P, TJ, HG], F32, attn_mem)
        rope_mem = ExitStack()
        ccos = sb("ccos", [P, 2, 2, BT], F32, rope_mem)
        csin = sb("csin", [P, 2, 2, BT], F32, rope_mem)
        rot = sb("rot", [P, 2, 2, BT], F32, rope_mem)
        res1 = sb("res1", [P, 2, 2, BT], F32, rope_mem)
        rope_mem.close()
        prob = sb("prob", [P, 4, HG, BT], F32, attn_mem)
        table_mem = ExitStack()
        cos_t = sb("cos_t", [P, S], F32, table_mem)
        sin_t = sb("sin_t", [P, S], F32, table_mem)
        piece = sb("piece", [P, 2, 2, PIECES, BT], BF16, table_mem)
        table_mem.close()
        attn_mem.close()

        aT = sb("aT", [P, 2, BT], F32)
        xh = sb("xh", [P, S], F32R)
        xl = sb("xl", [P, S], F32R)
        lg = sb("lg", [P, NT, NE], F32)
        ex = sb("ex", [P, NT, NE], F32)
        sc = sb("sc", [P, NT, NE], F32)
        mx = sb("mx", [P, NT], F32)
        sm = sb("sm", [P, NT], F32)
        rs = sb("rs", [P, NT], F32)
        top = sb("top", [P, NT, 8], F32)
        idx = sb("idx", [P, NT, 8], U32)
        idxf = sb("idxf", [P, NT, TOPK], F32)
        ts4 = sb("ts4", [P, NT], F32)
        tc4 = sb("tc4", [P, NT], F32)
        tr4 = sb("tr4", [P, NT], F32)
        w4 = sb("w4", [P, NT, TOPK], F32)
        hot = sb("hot", [P, NT, TOPK, NE], F32)
        hotw = sb("hotw", [P, NT, TOPK, NE], F32)
        wtok = sb("wtok", [P, NT, NE], F32)
        wTs = sb("wTs", [NE, S], F32)
        ewn = sb("ewn", [P, 2, 3, D], F32)
        ehi = sb("ehi", [P, 2, 2, D], F32R)
        elo = sb("elo", [P, 2, 2, D], F32R)
        edn = sb("edn", [P, 2, D], F32)
        wrow = sb("wrow", [1, 2, S], F32)
        wb = sb("wb", [P, 2, S], F32)
        th = sb("th", [P, 2, BT], F32)
        ga = sb("ga", [P, 2, BT], F32)
        hh = sb("hh", [P, 2, BT], F32)
        hw = sb("hw", [P, NJ, BT], F32)
        zb = sb("zb", [P, P], BF16)
        zr = sb("zr", [P, BT], BF16)
        fin = sb("fin", [P, NJ, BT], F32)
        yo = sb("yo", [P, NT, D], F32)

        bank = [ctx.enter_context(nc.psum_tensor(f"bank{i}", [P, 512], F32)) for i in range(2)]
        pair = [ctx.enter_context(nc.psum_tensor(f"pair{i}", [P, 2, 512], F32)) for i in range(2)]
        accb = ctx.enter_context(nc.psum_tensor("accb", [P, 512], F32))
        misc = ctx.enter_context(nc.psum_tensor("misc", [P, 512], F32))

        names = """w_in rw_in tab_in c_mem c_done c_cst st_done ag_done sq_done rc_done xn_done xt_pe xt_done
            wt_pe wt_act wt_dve qkv_pe v_pe v_done rp_dve rp_add rp_p1 rp_r1 rp_p2 rp_p3 stk_mem z_store
            stk_in vc_z vc_done mm_pe mx_rd mx_fin mt_pe ms_dve m_row qk_pe ex_act av_pe ot_act otT_pe rs_dve at_done
            a_pe a_act y_pe x2_dve st2 ag2 sq2 rc2 xn2 xt2_pe xh_act xl_dve xf_act lg_pe r_dve r_act
            wx_pe wx_dve w_st half_st half_m et_pe eh_act el_dve gu_pe th_act ga_dve hh_dve hw_pool wb_pool dn_pe
            ew_z fin_act ft_pe yo_dve o_st acc0 rs_out""".split()
        s = {n: sem(n) for n in names}
        x_in_s = [sem(f"x_in{J}") for J in range(NJ)]
        p_store = [sem(f"p_store{J}") for J in range(NJ)]
        ew_in = [sem(f"ew_in{k}") for k in range(2)]
        wr_in = [sem(f"wr_in{k}") for k in range(2)]

        block = ctx.enter_context(nc.Block())

        def tok(J):
            return slice(J * BT, (J + 1) * BT)

        def steps_with_maxima(G, engine_max, engine_event, engine_exp, engine_end, last):
            for u in range(NSTEP):
                q = u + LEAD
                nxt = q >= NSTEP
                if not (nxt and last):
                    engine_max(G + 1 if nxt else G, q % NSTEP, 0)
                engine_exp(G, u)
                if not (nxt and last):
                    engine_max(G + 1 if nxt else G, q % NSTEP, 1)
                for J in range(NJ):
                    if q == ENDS[J] + 1:
                        engine_event(G, J)
                    if q - NSTEP == ENDS[J] + 1 and not last:
                        engine_event(G + 1, J)
            engine_end(G)

        def lead_in(engine_max, engine_event):
            for q in range(LEAD):
                engine_max(0, q, 0)
                engine_max(0, q, 1)
                for J in range(NJ):
                    if q == ENDS[J] + 1:
                        engine_event(0, J)

        def over_groups(eng, body):
            for G in range(NG):
                body(G, G == NG - 1)

        @block.sync
        def _(sp):
            for J in range(NJ):
                sp.dma_start(xs[:, J * TJ:(J + 1) * TJ, :],
                             x_in[0, tok(J), :].rearrange("(t p) d -> p t d", p=P)).then_inc(x_in_s[J], 16)
            sp.dma_start(cos_t[:], cos_in).then_inc(s["tab_in"], 16)
            sp.dma_start(sin_t[:], sin_in).then_inc(s["tab_in"], 16)
            sp.wait_ge(s["half_m"], 1)
            sp.dma_start(wt_d[0:NSH, :], half[:]).then_inc(s["half_st"], 16)
            sp.wait_ge(s["stk_mem"], 4)
            sp.dma_start(zero_d, qst[96:96 + PIECES, 0].rearrange("p j h s -> p (j h s)")).then_inc(s["z_store"], 16)
            for J in range(NJ):
                for side, dst in ((0, qp_d), (1, kp_d)):
                    sp.wait_ge(s["rp_p3"], 2 * J + side + 1)
                    sp.dma_start(dst[J, 0:PIECES].rearrange("c p s -> p c s"),
                                 piece[:, J % 2, side, :, :]).then_inc(p_store[J], 16)
                sp.dma_start(kp_d[J, PIECES:].rearrange("c p s -> p c s"),
                             piece[:, J % 2, 1, 0:PIECES - 1, :]).then_inc(p_store[J], 16)
            for J in range(NJ):
                sp.wait_ge(p_store[J], 16 * 3)
            sp.wait_ge(s["z_store"], 16)

            def load_stacks(G):
                par = G % 2
                for r in range(REPS):
                    rows = slice(r * PIECES * DK, (r + 1) * PIECES * DK)
                    for dst, src, c0 in ((qst, qp_d, 0), (kst, kp_d, r)):
                        sp.dma_start(
                            dst[rows, bass.ds(par, 1)].rearrange("q a j h s -> q (a j) (h s)"),
                            src[:, c0:c0 + PIECES].rearrange("j c (r h) s -> (c r) j (h s)", h=NH)
                            [:, :, bass.ds(G * (HG * BT), HG * BT)]).then_inc(s["stk_in"], 16)
                sp.dma_start(qst[MROW:MROW + PIECES, bass.ds(par, 1)].rearrange("p a j h s -> p (a j h s)"),
                             zero_d).then_inc(s["stk_in"], 16)

            def store_m(n):
                G, J = n
                sp.wait_ge(s["ms_dve"], G * NJ + (J + 1))
                for c in range(PIECES):
                    sp.dma_start(qst[MROW + c:MROW + c + 1, bass.ds(G % 2, 1), J].rearrange("c a h s -> c (a h s)"),
                                 mp[:, c, :]).then_inc(s["m_row"], 16)

            load_stacks(0)
            sp.wait_ge(s["stk_in"], 16 * (2 * REPS + 1))

            def sp_group(G, last):
                if not last:
                    sp.wait_ge(s["av_pe"], G * NSTEP)
                    load_stacks(G + 1)
                store_m((G, 2))
                store_m((G, 3))
                if not last:
                    store_m((G + 1, 0))
                    store_m((G + 1, 1))

            store_m((0, 0))
            store_m((0, 1))
            over_groups(sp, sp_group)

            def expert_weights(buf, g, u, d):
                for k, w in enumerate((g, u, d)):
                    sp.dma_start(ewn[:, buf, k, :], w).then_inc(ew_in[buf], 16)

            def row(buf, w):
                sp.dma_start(wrow[:, buf, :], w).then_inc(wr_in[buf], 16)

            sp.wait_ge(s["at_done"], NG * NJ)
            sp.wait_ge(s["half_st"], 16)
            for c in range(NSH):
                if c >= 2:
                    sp.wait_ge(s["et_pe"], c - 1)
                    sp.wait_ge(s["wb_pool"], c - 1)
                h = slice(c * D, (c + 1) * D)
                expert_weights(c % 2, sg_in[h, :], su_in[h, :], sd_in[:, h])
                row(c % 2, wt_d[c:c + 1, :])
            sp.wait_ge(s["wx_dve"], NJ)
            sp.dma_start(wt_d[NSH:, :], wTs[:]).then_inc(s["w_st"], 16)
            sp.wait_ge(s["w_st"], 16)
            with sp.Fori(0, NE // 2) as i:
                for k in range(2):
                    e = 2 * i
                    sp.wait_ge(s["et_pe"], e + (NSH + k - 1))
                    sp.wait_ge(s["wb_pool"], e + (NSH + k - 1))
                    one = bass.ds(e + k, 1)
                    expert_weights(k, *(w[one, :, :].rearrange("a p d -> (a p) d") for w in (gw_in, uw_in, dw_in)))
                    row(k, wt_d[bass.ds(e + (NSH + k), 1), :])
            sp.wait_ge(s["et_pe"], NX - 1)
            sp.wait_ge(s["wb_pool"], NX - 1)
            expert_weights(0, gw_in[0], uw_in[0], dw_in[0])
            row(0, wt_d[0:1, :])
            for J in range(NJ):
                sp.wait_ge(s["yo_dve"], J + 1)
                sp.dma_start(out[0, tok(J), :].rearrange("(t p) d -> p t d", p=P),
                             yo[:, J * TJ:(J + 1) * TJ, :]).then_inc(s["o_st"], 16)
            sp.wait_ge(s["o_st"], 16 * NJ)

        @block.gpsimd
        def _(pool):
            pool.memset(ident[:], 0.0).then_inc(s["c_mem"], 1)
            pool.memset(negI[:], 0.0).then_inc(s["c_mem"], 1)
            pool.memset(later_k[:], 1.0).then_inc(s["c_mem"], 1)
            pool.memset(later_p[:], 1.0).then_inc(s["c_mem"], 1)
            pool.wait_ge(s["c_mem"], 4)
            pool.affine_select(out=ident[:], in_=ident[:], compare_op=ALU.not_equal, fill=1.0, base=0,
                               pattern=[[-1, P]], channel_multiplier=1).then_inc(s["c_done"], 1)
            pool.affine_select(out=negI[:], in_=negI[:], compare_op=ALU.not_equal, fill=-BIG, base=0,
                               pattern=[[-1, P]], channel_multiplier=1).then_inc(s["c_done"], 1)
            pool.affine_select(out=later_k[:], in_=later_k[:], compare_op=ALU.is_gt, fill=0.0, base=0,
                               pattern=[[1, P]], channel_multiplier=-1).then_inc(s["c_done"], 1)
            pool.affine_select(out=later_p[:], in_=later_p[:], compare_op=ALU.is_gt, fill=0.0, base=0,
                               pattern=[[-1, P]], channel_multiplier=1).then_inc(s["c_done"], 1)
            pool.iota(iota_i[:], pattern=[[1, NE]], base=0, channel_multiplier=0).then_inc(s["c_done"], 1)
            pool.memset(half[:], 0.5).then_inc(s["half_m"], 1)
            pool.wait_ge(s["c_done"], 5)
            pool.wait_ge(s["half_m"], 1)
            for par in range(2):
                pool.memset(qst[64:P, par, :, :], 0.0).then_inc(s["stk_mem"], 1)
                pool.memset(kst[64:P, par, :, :], 1.0).then_inc(s["stk_mem"], 1)
            pool.wait_ge(s["stk_mem"], 4)
            pool.memset(vcur[:], 0.0).then_inc(s["vc_z"], 1)
            pool.memset(vext[:, :, :, DK:DK + 1], 1.0).then_inc(s["vc_z"], 1)
            for J in range(NJ):
                for side in range(2):
                    pool.wait_ge(s["rp_dve"], 2 * J + side + 1)
                    if J >= 2:
                        pool.wait_ge(s["rp_r1"], 2 * (J - 2) + side + 1)
                    pool.tensor_tensor(rot[:, J % 2, side, :], ccos[:, J % 2, side, :], csin[:, J % 2, side, :],
                                       ALU.add).then_inc(s["rp_add"], 1)
            pool.wait_ge(s["vc_z"], 2)
            pool.wait_ge(s["v_done"], NJ)

            def pool_group(G, last):
                pool.wait_ge(s["av_pe"], G * NSTEP)
                pool.tensor_copy(vcur[:, :, :, 0:DK + 1], vext[:, :, bass.ds(G * HG, HG), :]).then_inc(s["vc_done"], 1)

            over_groups(pool, pool_group)

            pool.wait_ge(s["at_done"], NG * NJ)
            pool.memset(zb[:], 0.0).then_inc(s["ew_z"], 1)
            pool.memset(zr[:], 0.0).then_inc(s["ew_z"], 1)
            pool.memset(edn[:, 1, :], 0.0).then_inc(s["ew_z"], 1)
            for J in (NJ - 2, NJ - 1):
                pool.memset(hw[:, J, :], 0.0).then_inc(s["hw_pool"], 1)

            def row_ready(i, e, buf):
                pool.wait_ge(wr_in[buf], 16 * i + 16)
                pool.wait_ge(s["hw_pool"], e * NJ - 2)

            def spread(buf):
                pool.partition_broadcast(wb[:, buf, :], wrow[:, buf, :]).then_inc(s["wb_pool"], 1)

            def weigh(e, buf, J):
                n = e * NJ + J
                pool.wait_ge(s["hh_dve"], n + 3)
                if J == 0:
                    pool.wait_ge(s["wb_pool"], e + 1)
                pool.wait_ge(s["dn_pe"], n + 1)
                pool.tensor_tensor(hw[:, J, :], hh[:, J % 2, :], wb[:, buf, tok(J)], ALU.mult)\
                    .then_inc(s["hw_pool"], 1)

            pool.wait_ge(wr_in[0], 16)
            pool.partition_broadcast(wb[:, 0, :], wrow[:, 0, :]).then_inc(s["wb_pool"], 1)
            with pool.Fori(0, NX // 2) as i:
                for k in range(2):
                    weigh(2 * i + k, k, 0)
                    row_ready(i + k, 2 * i + (k + 1), 1 - k)
                    weigh(2 * i + k, k, 1)
                    spread(1 - k)
                    weigh(2 * i + k, k, 2)
                    weigh(2 * i + k, k, 3)

        @block.scalar
        def _(act):
            for k, w in enumerate((wq_in, wk_in, wv_in, wo_in)):
                act.dma_start(wnat[:, k, :], w).then_inc(s["w_in"], 16)
            act.dma_start(rwn[:], rw_in).then_inc(s["rw_in"], 16)
            act.dma_start(bias[:], rb_in.rearrange("(a e) -> a e", a=1).to_broadcast([P, NE])).then_inc(s["rw_in"], 16)

            act.wait_ge(s["c_cst"], 1)
            for J in range(NJ):
                act.wait_ge(s["ag_done"], TJ * (J + 1))
                act.activation(std[:, J * TJ:(J + 1) * TJ], mv[:, J * TJ:(J + 1) * TJ, 1], ACT.Sqrt,
                               bias=eps[:, 0:1]).then_inc(s["sq_done"], 1)
            act.wait_ge(s["wt_pe"], 4)
            for k in range(2):
                src = bank[1][:, k * D:(k + 1) * D]
                act.activation(wT[:, 2 * k, :].rearrange("p (r h) -> p h r", h=NH),
                               src.rearrange("p (h r) -> p h r", h=NH), ACT.Copy).then_inc(s["wt_act"], 1)
                for a in range(2):
                    act.activation(wT[:, 2 * k + 1, a * (D // 2):(a + 1) * (D // 2)].rearrange("p (r h) -> p h r", h=NH),
                                   src.rearrange("p (h a r) -> p h a r", h=NH, a=2)[:, :, 1 - a, :], ACT.Copy)\
                        .then_inc(s["wt_act"], 1)
            act.activation(wT[:, 4:6, :].rearrange("p a d -> p (a d)"), bank[1][:, 2 * D:4 * D], ACT.Copy)\
                .then_inc(s["wt_act"], 1)

            for J in range(NJ):
                act.wait_ge(s["xt_pe"], J + 1)
                act.activation(xnT[:, tok(J)], bank[0][:], ACT.Copy).then_inc(s["xt_done"], 1)
                act.wait_ge(s["v_pe"], J + 1)
                act.wait_ge(s["vc_z"], 2)
                act.activation(vext[:, J * TJ:(J + 1) * TJ, :, 0:DK],
                               misc[:].rearrange("p (t h r) -> p t h r", t=TJ, h=NH), ACT.Copy).then_inc(s["v_done"], 1)
                if J >= 2:
                    act.wait_ge(p_store[J - 2], 16 * 3)
                for side in range(2):
                    act.wait_ge(s["rp_add"], 2 * J + side + 1)
                    act.activation(piece[:, J % 2, side, 0, :], rot[:, J % 2, side, :], ACT.Copy).then_inc(s["rp_p1"], 1)
                for side in range(2):
                    act.wait_ge(s["rp_r1"], 2 * J + side + 1)
                    act.activation(piece[:, J % 2, side, 1, :], res1[:, J % 2, side, :], ACT.Copy).then_inc(s["rp_p2"], 1)

            def act_exp(G, u):
                J, t = STEPS[u]
                c0 = max(t - TJ * J, 0) * P
                for p in range(2):
                    act.wait_ge(s["qk_pe"], G * (2 * NSTEP) + (2 * u + p + 1))
                    if u >= 4:
                        act.wait_ge(s["av_pe"], G * NSTEP + (u - 3))
                    act.activation(prob[:, u % 4, 2 * p:2 * p + 2, c0:], pair[p][:, :, c0:], ACT.Exp, scale=SCALE)\
                        .then_inc(s["ex_act"], 1)
                if u in ENDS:
                    act_evac(G, ENDS.index(u))

            def act_evac(G, J):
                act.wait_ge(s["av_pe"], G * NSTEP + ENDS[J])
                if not (isinstance(G, int) and G == 0 and J == 0):
                    act.wait_ge(s["otT_pe"], G * NJ + J)
                act.activation(ot[:], accb[:], ACT.Copy).then_inc(s["ot_act"], 1)

            def nothing(*a):
                return None

            def act_group(G, last):
                steps_with_maxima(G, nothing, nothing, act_exp, lambda g: act_evac(g, NJ - 1), last)

            act.wait_ge(s["rp_p3"], 2 * NJ)
            over_groups(act, act_group)

            for J in range(NJ):
                act.wait_ge(s["a_pe"], J + 1)
                if J >= 2:
                    act.wait_ge(s["y_pe"], J - 1)
                act.activation(aT[:, J % 2, :], bank[0][:], ACT.Copy).then_inc(s["a_act"], 1)
            for J in range(NJ):
                act.wait_ge(s["ag2"], TJ * (J + 1))
                act.activation(std[:, J * TJ:(J + 1) * TJ], mv[:, J * TJ:(J + 1) * TJ, 1], ACT.Sqrt,
                               bias=eps[:, 0:1]).then_inc(s["sq2"], 1)
            for J in range(NJ):
                act.wait_ge(s["xt2_pe"], J + 1)
                act.activation(xh[:, tok(J)], bank[J % 2][:], ACT.Copy).then_inc(s["xh_act"], 1)
                act.activation(xnT[:, tok(J)], bank[J % 2][:], ACT.Copy).then_inc(s["xf_act"], 1)
            act.wait_ge(s["r_dve"], 3)
            act.activation(ex[:], sc[:], ACT.Exp).then_inc(s["r_act"], 1)

            def turned_weights(e, buf, slot):
                act.wait_ge(s["et_pe"], e + 1)
                act.activation(ehi[:, buf, :, :].rearrange("p a d -> p (a d)"), pair[slot][:, 0, 0:2 * D], ACT.Copy)\
                    .then_inc(s["eh_act"], 1)
                act.activation(edn[:, buf, :], pair[slot][:, 1, 0:D], ACT.Copy).then_inc(s["eh_act"], 1)

            def gate(e, J, slot):
                n = e * NJ + J
                act.wait_ge(s["gu_pe"], n + 1)
                act.wait_ge(s["ga_dve"], n + 1)
                act.activation(th[:, J % 2, :], pair[slot][:, 0, :], ACT.Tanh, scale=0.5).then_inc(s["th_act"], 1)

            act.wait_ge(s["ew_z"], 3)
            turned_weights(0, 0, 1)
            with act.Fori(0, NX // 2) as i:
                for k in range(2):
                    e = 2 * i
                    gate(e + k, 0, k)
                    gate(e + k, 1, 1 - k)
                    gate(e + k, 2, k)
                    turned_weights(e + (k + 1), 1 - k, 1 - k)
                    gate(e + k, 3, k)
            for J in range(NJ):
                act.wait_ge(s["acc0"], 1)
                act.activation(fin[:, J, :], [accb, misc, bank[0], bank[1]][J][:], ACT.Copy).then_inc(s["fin_act"], 1)

        @block.tensor
        def _(pe):
            def mm(out, a, b, start=True, stop=True, loose=False):
                return nc.tensor.matmul(out, a, b, start=start, stop=stop, skip_group_check=loose)

            pe.wait_ge(s["c_done"], 5)
            pe.wait_ge(s["w_in"], 16 * 4)
            for k in range(4):
                nc.tensor.transpose(bank[1][:, k * D:(k + 1) * D], wnat[:, k, :], ident[:]).then_inc(s["wt_pe"], 1)
            pe.wait_ge(s["wt_act"], 7)
            pe.wait_ge(s["rw_in"], 32)
            nc.tensor.transpose(bank[1][:, 0:NE], rwn[:], ident[0:NE, 0:NE]).then_inc(s["wt_pe"], 1)

            for J in range(NJ):
                pe.wait_ge(s["xn_done"], TJ * (J + 1))
                if J:
                    pe.wait_ge(s["xt_done"], J)
                for i in range(TJ):
                    last = nc.tensor.transpose(bank[0][:, i * P:(i + 1) * P], xn[:, J * TJ + i, :], ident[:])
                last.then_inc(s["xt_pe"], 1)
                pe.wait_ge(s["xt_done"], J + 1)
                for side in range(2):
                    if J:
                        pe.wait_ge(s["rp_dve"], 2 * (J - 1) + side + 1)
                    mm(pair[side][:, 0, :], wT[:, 2 * side, :], xnT[:, tok(J)])
                    mm(pair[side][:, 1, :], wT[:, 2 * side + 1, :], xnT[:, tok(J)]).then_inc(s["qkv_pe"], 1)
                if J:
                    pe.wait_ge(s["v_done"], J)
                for i in range(TJ):
                    last = mm(misc[:, i * P:(i + 1) * P], xnT[:, J * BT + i * P:J * BT + (i + 1) * P], wT[:, 4, :])
                last.then_inc(s["v_pe"], 1)

            PER = HG * NSTEP

            def pe_max(G, q, part):
                J, i, c = MAXES[q]
                n = (i + 1) * P if c == J else BT
                par = G % 2
                for h in (0, 1) if part == 0 else (2, 3):
                    k = HG * q + h
                    if not (isinstance(G, int) and G == 0 and k < 2):
                        pe.wait_ge(s["mx_rd"], G * PER + (k - 1))
                    last = mm(bank[h % 2][:, 0:n], qst[:, bass.ds(par, 1), J, h, i * P:(i + 1) * P],
                              kst[:, bass.ds(par, 1), c, h, 0:n], stop=c != J)
                    if c == J:
                        last = mm(bank[h % 2][:, i * P:n], negI[:], later_k[:], start=False)
                    last.then_inc(s["mm_pe"], 1)

            def pe_event(G, J):
                n = G * NJ + J
                pe.wait_ge(s["mx_fin"], n + 1)
                if not isinstance(n, int) or n >= 2:
                    pe.wait_ge(s["ms_dve"], n)
                    pe.wait_ge(s["at_done"], n - 1 if J == NJ - 1 else n - 2)
                nc.tensor.transpose(misc[0:HG * TJ, 0:P], negm[:], ident[:]).then_inc(s["mt_pe"], 1)

            def pe_av(G, u):
                J, t = STEPS[u]
                c0 = max(t - TJ * J, 0) * P
                pe.wait_ge(s["ex_act"], G * (2 * NSTEP) + (2 * u + 2))
                if t == 0 and not (isinstance(G, int) and G == 0 and J == 0):
                    pe.wait_ge(s["ot_act"], G * NJ + J)
                if u == 0:
                    pe.wait_ge(s["vc_done"], G + 1)
                for h in range(HG):
                    last = mm(accb[32 * h:32 * h + 32, c0:], vcur[:, t, h, :], prob[:, u % 4, h, c0:],
                              start=t == 0, stop=t == TJ * (J + 1) - 1)
                last.then_inc(s["av_pe"], 1)

            def pe_out(G, J):
                n = G * NJ + J
                pe.wait_ge(s["ot_act"], n + 1)
                pe.wait_ge(s["at_done"], n)
                before = n + (2 if J == 1 else 3)
                pe.wait_ge(s["ms_dve"], min(before, NG * NJ) if isinstance(n, int) else before)
                for i in range(TJ):
                    last = nc.tensor.transpose(misc[:, i * P:(i + 1) * P], ot[:, i * P:(i + 1) * P], ident[:])
                last.then_inc(s["otT_pe"], 1)

            def pe_exp(G, u):
                J, t = STEPS[u]
                d = t - TJ * J
                c0 = max(d, 0) * P
                par = G % 2
                if t == 0:
                    pe.wait_ge(s["m_row"], 16 * PIECES * (G * NJ + (J + 1)))
                for p in range(2):
                    k = 2 * u + p
                    if k >= 2:
                        pe.wait_ge(s["ex_act"], G * (2 * NSTEP) + (k - 1))
                    for h in range(2):
                        last = mm(pair[p][:, h, c0:], kst[:, bass.ds(par, 1), t // TJ, 2 * p + h, t % TJ * P:(t % TJ + 1) * P],
                                  qst[:, bass.ds(par, 1), J, 2 * p + h, c0:], stop=d < 0)
                        if d >= 0:
                            last = mm(pair[p][:, h, c0:c0 + P], negI[:], later_p[:], start=False)
                    last.then_inc(s["qk_pe"], 1)
                if u:
                    pe_av(G, u - 1)
                for b in range(NJ):
                    if u == ENDS[b] + 1:
                        pe_out(G, b)

            def pe_end(G):
                pe_av(G, NSTEP - 1)
                pe_out(G, NJ - 1)

            def pe_group(G, last):
                steps_with_maxima(G, pe_max_waited, pe_event, pe_exp, pe_end, last)

            def pe_max_waited(G, q, part):
                if q == 0 and part == 0:
                    pe.wait_ge(s["stk_in"], 16 * (2 * REPS + 1) * (G + 1))
                pe_max(G, q, part)

            pe.wait_ge(s["rp_dve"], 2 * NJ)
            pe.wait_ge(s["v_done"], NJ)
            pe.wait_ge(s["wt_dve"], 1)
            pe.wait_ge(s["xt_done"], NJ)
            pe.wait_ge(s["stk_mem"], 4)
            lead_in(pe_max_waited, pe_event)
            over_groups(pe, pe_group)

            pe.wait_ge(s["mx_rd"], NG * PER)
            pe.wait_ge(s["at_done"], NG * NJ)
            for J in range(NJ):
                if J:
                    pe.wait_ge(s["a_act"], J)
                for i in range(TJ):
                    last = nc.tensor.transpose(bank[0][:, i * P:(i + 1) * P], attn[:, J * TJ + i, :], ident[:])
                last.then_inc(s["a_pe"], 1)
                pe.wait_ge(s["a_act"], J + 1)
                if J:
                    pe.wait_ge(s["x2_dve"], J)
                for i in range(TJ):
                    last = mm(bank[1][:, i * P:(i + 1) * P], aT[:, J % 2, i * P:(i + 1) * P], wT[:, 5, :])
                last.then_inc(s["y_pe"], 1)
            pe.wait_ge(s["x2_dve"], NJ)
            for J in range(NJ):
                pe.wait_ge(s["xn2"], TJ * (J + 1))
                if J >= 2:
                    pe.wait_ge(s["xl_dve"], J - 1)
                    pe.wait_ge(s["xf_act"], J - 1)
                for i in range(TJ):
                    last = nc.tensor.transpose(bank[J % 2][:, i * P:(i + 1) * P], xn[:, J * TJ + i, :], ident[:])
                last.then_inc(s["xt2_pe"], 1)
            for J in range(NJ):
                pe.wait_ge(s["xf_act"], J + 1)
                for i in range(TJ):
                    t = J * TJ + i
                    last = mm(misc[:, t * NE:(t + 1) * NE], xnT[:, t * P:(t + 1) * P], rwT[:])
            last.then_inc(s["lg_pe"], 1)
            pe.wait_ge(s["r_dve"], 17)
            for J in range(NJ):
                for i in range(TJ):
                    t = J * TJ + i
                    last = nc.tensor.transpose(pair[J // 2][0:NE, J % 2, i * P:(i + 1) * P], wtok[:, t, :], ident[:])
                last.then_inc(s["wx_pe"], 1)

            out_bank = [accb, misc, bank[0], bank[1]]
            pe.wait_ge(s["wx_dve"], NJ)
            pe.wait_ge(s["xl_dve"], NJ)
            pe.wait_ge(s["ew_z"], 3)
            for J in range(NJ):
                last = mm(out_bank[J][:], zb[:], zr[:], stop=False, loose=True)
                if J < 2:
                    last.then_inc(s["dn_pe"], 1)

            def turn(i, buf, slot):
                pe.wait_ge(ew_in[buf], 48 * i + 48)
                for k in range(3):
                    last = nc.tensor.transpose(pair[slot][:, k // 2, (k % 2) * D:(k % 2 + 1) * D], ewn[:, buf, k, :], ident[:])
                last.then_inc(s["et_pe"], 1)

            def gate_up(e, buf, J, slot):
                n = e * NJ + J
                if J == 0:
                    pe.wait_ge(s["eh_act"], 2 * e + 2)
                    pe.wait_ge(s["el_dve"], e + 1)
                for k in range(2):
                    o = pair[slot][:, k, :]
                    mm(o, ehi[:, buf, k, :], xh[:, tok(J)], stop=False)
                    mm(o, ehi[:, buf, k, :], xl[:, tok(J)], start=False, stop=False)
                    last = mm(o, elo[:, buf, k, :], xh[:, tok(J)], start=False)
                last.then_inc(s["gu_pe"], 1)

            def down(n, buf, J):
                pe.wait_ge(s["hw_pool"], n + 1)
                mm(out_bank[J][:], edn[:, buf, :], hw[:, J, :], start=False, stop=False, loose=True)\
                    .then_inc(s["dn_pe"], 1)

            turn(0, 0, 1)
            with pe.Fori(0, NX // 2) as i:
                for k in range(2):
                    e = 2 * i + k
                    n = e * NJ
                    gate_up(e, k, 0, k)
                    down(n, 1 - k, NJ - 2)
                    pe.wait_ge(s["hh_dve"], n + 2)
                    gate_up(e, k, 1, 1 - k)
                    down(n + 1, 1 - k, NJ - 1)
                    pe.wait_ge(s["hh_dve"], n + 3)
                    gate_up(e, k, 2, k)
                    down(n + 2, k, 0)
                    pe.wait_ge(s["hh_dve"], n + 4)
                    turn(i + k, 1 - k, 1 - k)
                    pe.wait_ge(s["hh_dve"], n + 5)
                    gate_up(e, k, 3, k)
                    down(n + 3, k, 1)
            for J in (NJ - 2, NJ - 1):
                down(NX * NJ + J - (NJ - 2), 1, J)
            for J in range(NJ):
                last = mm(out_bank[J][:], zb[:], zr[:], start=False, loose=True)
            last.then_inc(s["acc0"], 1)
            pe.wait_ge(s["eh_act"], 2 * (NX + 1))
            pe.wait_ge(s["el_dve"], NX + 1)
            for J in range(NJ):
                pe.wait_ge(s["fin_act"], J + 1)
                for i in range(TJ):
                    last = nc.tensor.transpose(pair[J // 2][:, J % 2, i * P:(i + 1) * P], fin[:, J, i * P:(i + 1) * P], ident[:])
                last.then_inc(s["ft_pe"], 1)

        @block.vector
        def _(dve):
            dve.memset(eps[:], EPS).then_inc(s["c_cst"], 1)

            def layernorm(st, ag, sq, rc, done, ready):
                for J in range(NJ):
                    ready(J)
                    for i in range(TJ):
                        t = J * TJ + i
                        dve.bn_stats(stats[:, t, :], xs[:, t, :]).then_inc(s[st], 1)
                    for i in range(TJ):
                        t = J * TJ + i
                        dve.wait_ge(s[st], t + 1)
                        dve.bn_aggr(mv[:, t, :], stats[:, t, :]).then_inc(s[ag], 1)
                for J in range(NJ):
                    dve.wait_ge(s[sq], J + 1)
                    dve.reciprocal(rstd[:, J * TJ:(J + 1) * TJ], std[:, J * TJ:(J + 1) * TJ]).then_inc(s[rc], 1)
                    dve.wait_ge(s[rc], J + 1)
                    for i in range(TJ):
                        t = J * TJ + i
                        dve.tensor_scalar(xn[:, t, :], xs[:, t, :], mv[:, t, 0:1], rstd[:, t:t + 1],
                                          ALU.subtract, ALU.mult).then_inc(s[done], 1)

            layernorm("st_done", "ag_done", "sq_done", "rc_done", "xn_done",
                      lambda J: dve.wait_ge(x_in_s[J], 16))
            dve.wait_ge(s["wt_pe"], 5)
            dve.tensor_copy(rwT[:], bank[1][:, 0:NE]).then_inc(s["wt_dve"], 1)
            dve.wait_ge(s["tab_in"], 32)
            for J in range(NJ):
                for side in range(2):
                    dve.wait_ge(s["qkv_pe"], 2 * J + side + 1)
                    if J >= 2:
                        dve.wait_ge(s["rp_add"], 2 * (J - 2) + side + 1)
                    dve.tensor_tensor(ccos[:, J % 2, side, :], pair[side][:, 0, :], cos_t[:, tok(J)], ALU.mult)
                    dve.tensor_tensor(csin[:, J % 2, side, :], pair[side][:, 1, :], sin_t[:, tok(J)], ALU.mult)\
                        .then_inc(s["rp_dve"], 1)
                for side in range(2):
                    dve.wait_ge(s["rp_p1"], 2 * J + side + 1)
                    if J >= 2:
                        dve.wait_ge(s["rp_p2"], 2 * (J - 2) + side + 1)
                        dve.wait_ge(s["rp_p3"], 2 * (J - 2) + side + 1)
                    dve.tensor_tensor(res1[:, J % 2, side, :], rot[:, J % 2, side, :], piece[:, J % 2, side, 0, :],
                                      ALU.subtract).then_inc(s["rp_r1"], 1)
                if J >= 2:
                    dve.wait_ge(p_store[J - 2], 16 * 3)
                for side in range(2):
                    dve.wait_ge(s["rp_p2"], 2 * J + side + 1)
                    dve.wait_ge(s["rp_r1"], 2 * J + side + 1)
                    dve.tensor_tensor(piece[:, J % 2, side, 2, :], res1[:, J % 2, side, :], piece[:, J % 2, side, 1, :],
                                      ALU.subtract).then_inc(s["rp_p3"], 1)

            PER = HG * NSTEP

            def dve_max(G, q, part):
                J, i, c = MAXES[q]
                n = (i + 1) * P if c == J else BT
                if part == 0 and i == 0 and c == 0 and not (isinstance(G, int) and G == 0 and J == 0):
                    dve.wait_ge(s["mx_fin"], G * NJ + J)
                for h in (0, 1) if part == 0 else (2, 3):
                    dve.wait_ge(s["mm_pe"], G * PER + (HG * q + h + 1))
                    dve.tensor_reduce(pmax[:, h, i, c:c + 1], bank[h % 2][:, 0:n], AX, ALU.max).then_inc(s["mx_rd"], 1)
                if part == 1 and (i, c) == (TJ - 1, J):
                    dve.wait_ge(s["mx_rd"], G * PER + HG * (q + 1))
                    if not (isinstance(G, int) and G == 0 and J == 0):
                        dve.wait_ge(s["mt_pe"], G * NJ + J)
                    dve.tensor_reduce(negm[:], pmax[:, :, :, 0:J + 1].rearrange("p h i c -> p (h i) c"), AX,
                                      ALU.max, negate=True).then_inc(s["mx_fin"], 1)

            def dve_event(G, J):
                k = G * NJ + J
                dve.wait_ge(s["mt_pe"], k + 1)
                if not (isinstance(k, int) and k == 0):
                    dve.wait_ge(s["m_row"], 16 * PIECES * k)
                row = misc[0:HG * TJ, 0:P]
                dve.tensor_copy(mp[:, 0, :], row).then_inc(s["rs_dve"], 1)
                dve.wait_ge(s["rs_dve"], 4 * k + 1)
                dve.tensor_tensor(mres[:, 0, :], row, mp[:, 0, :], ALU.subtract).then_inc(s["rs_dve"], 1)
                dve.wait_ge(s["rs_dve"], 4 * k + 2)
                dve.tensor_copy(mp[:, 1, :], mres[:, 0, :]).then_inc(s["rs_dve"], 1)
                dve.wait_ge(s["rs_dve"], 4 * k + 3)
                dve.tensor_tensor(mres[:, 1, :], mres[:, 0, :], mp[:, 1, :], ALU.subtract).then_inc(s["rs_dve"], 1)
                dve.wait_ge(s["rs_dve"], 4 * k + 4)
                dve.tensor_copy(mp[:, 2, :], mres[:, 1, :]).then_inc(s["ms_dve"], 1)

            def dve_out(G, J):
                k = G * NJ + J
                dve.wait_ge(s["otT_pe"], k + 1)
                rows = misc[:].rearrange("p (i h r) -> p i h r", i=TJ, h=HG)
                if not (isinstance(k, int) and k == 0):
                    dve.wait_ge(s["at_done"], k)
                dve.reciprocal(rsum[:], rows[:, :, :, DK]).then_inc(s["rs_out"], 1)
                dve.wait_ge(s["rs_out"], k + 1)
                dst = attn[:, J * TJ:(J + 1) * TJ, :].rearrange("p i (g h r) -> p i g h r", g=NG, h=HG)
                for i in range(TJ):
                    last = dve.tensor_tensor(dst[:, i, bass.ds(G, 1), :, :].rearrange("p a h r -> p (a h) r"),
                                             rows[:, i, :, 0:DK],
                                             rsum[:, i, :].unsqueeze(2).to_broadcast([P, HG, DK]), ALU.mult)
                last.then_inc(s["at_done"], 1)

            def dve_exp(G, u):
                for b in range(NJ):
                    if u == ENDS[b] + 1:
                        dve_out(G, b)

            def dve_group(G, last):
                steps_with_maxima(G, dve_max, dve_event, dve_exp, lambda g: dve_out(g, NJ - 1), last)

            lead_in(dve_max, dve_event)
            over_groups(dve, dve_group)

            for J in range(NJ):
                dve.wait_ge(s["y_pe"], J + 1)
                cols = slice(J * TJ, (J + 1) * TJ)
                dve.tensor_tensor(xs[:, cols, :], xs[:, cols, :], bank[1][:].rearrange("p (i d) -> p i d", i=TJ),
                                  ALU.add).then_inc(s["x2_dve"], 1)
            layernorm("st2", "ag2", "sq2", "rc2", "xn2", lambda J: dve.wait_ge(s["x2_dve"], J + 1))
            for J in range(NJ):
                dve.wait_ge(s["xh_act"], J + 1)
                dve.wait_ge(s["xf_act"], J + 1)
                dve.tensor_tensor(xl[:, tok(J)], bank[J % 2][:], xh[:, tok(J)].bitcast(F32), ALU.subtract)\
                    .then_inc(s["xl_dve"], 1)

            count = [0]

            def step(ins):
                ins.then_inc(s["r_dve"], 1)
                count[0] += 1
                dve.wait_ge(s["r_dve"], count[0])

            def over(a, shape):
                return a.to_broadcast(shape)

            full = [P, NT, NE]
            dve.wait_ge(s["lg_pe"], 1)
            dve.wait_ge(s["rw_in"], 32)
            step(dve.tensor_tensor(lg[:], misc[:].rearrange("p (t e) -> p t e", t=NT), over(bias[:].unsqueeze(1), full), ALU.add))
            step(dve.tensor_reduce(mx[:], lg[:], AX, ALU.max))
            step(dve.tensor_tensor(sc[:], lg[:], over(mx[:].unsqueeze(2), full), ALU.subtract))
            dve.wait_ge(s["r_act"], 1)
            step(dve.tensor_reduce(sm[:], ex[:], AX, ALU.add))
            step(dve.reciprocal(rs[:], sm[:]))
            step(dve.tensor_tensor(lg[:], ex[:], over(rs[:].unsqueeze(2), full), ALU.mult))
            for t in range(NT):
                last = dve.max(top[:, t, :], lg[:, t, :])
            step(last)
            for t in range(NT):
                last = dve.max_index(idx[:, t, :], top[:, t, :], lg[:, t, :])
            step(last)
            step(dve.tensor_copy(idxf[:], idx[:, :, 0:TOPK]))
            step(dve.tensor_reduce(ts4[:], top[:, :, 0:TOPK], AX, ALU.add))
            step(dve.tensor_scalar(tc4[:], ts4[:], 1e-12, 2.0, ALU.max, ALU.mult))
            step(dve.reciprocal(tr4[:], tc4[:]))
            step(dve.tensor_tensor(w4[:], top[:, :, 0:TOPK], over(tr4[:].unsqueeze(2), [P, NT, TOPK]), ALU.mult))
            wide = [P, NT, TOPK, NE]
            step(dve.tensor_copy(iota_e[:], iota_i[:]))
            step(dve.tensor_tensor(hot[:], over(iota_e[:].unsqueeze(1).unsqueeze(1), wide), over(idxf[:].unsqueeze(3), wide),
                                   ALU.is_equal))
            step(dve.tensor_tensor(hotw[:], hot[:], over(w4[:].unsqueeze(3), wide), ALU.mult))
            step(dve.tensor_reduce(wtok[:], hotw[:].rearrange("p t j e -> p t e j"), AX, ALU.add))
            assert count[0] == 17
            for J in range(NJ):
                dve.wait_ge(s["wx_pe"], J + 1)
                dve.tensor_copy(wTs[:, tok(J)], pair[J // 2][0:NE, J % 2, :]).then_inc(s["wx_dve"], 1)

            def low_parts(e, buf, slot):
                dve.wait_ge(s["eh_act"], 2 * e + 1)
                dve.tensor_tensor(elo[:, buf, :, :].rearrange("p a d -> p (a d)"), pair[slot][:, 0, 0:2 * D],
                                  ehi[:, buf, :, :].rearrange("p a d -> p (a d)").bitcast(F32), ALU.subtract)\
                    .then_inc(s["el_dve"], 1)

            def hidden(e, J, slot):
                n = e * NJ + J
                b = J % 2
                dve.wait_ge(s["th_act"], n + 1)
                dve.wait_ge(s["hh_dve"], n + 1)
                dve.scalar_tensor_tensor(ga[:, b, :], th[:, b, :], 1.0, pair[slot][:, 0, :], ALU.add, ALU.mult)\
                    .then_inc(s["ga_dve"], 1)
                dve.wait_ge(s["ga_dve"], n + 3)
                dve.wait_ge(s["hw_pool"], n + 1)
                dve.tensor_tensor(hh[:, b, :], ga[:, b, :], pair[slot][:, 1, :], ALU.mult).then_inc(s["hh_dve"], 1)

            for b in range(2):
                dve.memset(ga[:, b, 0:1], 0.0).then_inc(s["ga_dve"], 1)
                dve.memset(hh[:, b, 0:1], 0.0).then_inc(s["hh_dve"], 1)
            low_parts(0, 0, 1)
            with dve.Fori(0, NX // 2) as i:
                for k in range(2):
                    e = 2 * i
                    hidden(e + k, 0, k)
                    hidden(e + k, 1, 1 - k)
                    hidden(e + k, 2, k)
                    low_parts(e + (k + 1), 1 - k, 1 - k)
                    hidden(e + k, 3, k)
            for J in range(NJ):
                cols = slice(J * TJ, (J + 1) * TJ)
                dve.wait_ge(s["ft_pe"], J + 1)
                dve.tensor_tensor(yo[:, cols, :], xs[:, cols, :],
                                  pair[J // 2][:, J % 2, :].rearrange("p (i d) -> p i d", i=TJ), ALU.add)\
                    .then_inc(s["yo_dve"], 1)


_INS = ["L0_attn_x", "L0_attn_W_Q", "L0_attn_W_K", "L0_attn_W_V", "L0_attn_W_O", "L0_ffn_router_w",
        "L0_ffn_router_bias", "L0_ffn_gate_w", "L0_ffn_up_w", "L0_ffn_down_w", "L0_ffn_sgate_w", "L0_ffn_sup_w",
        "L0_ffn_sdown_w"]


def rope_tables():
    theta = np.float32(1.0) / np.float32(10000.0) ** (np.arange(0, DK, 2, dtype=np.float32) / np.float32(DK))
    ang = np.outer(np.arange(S, dtype=np.float32), theta.astype(np.float32)).astype(np.float32)
    ang = np.concatenate([ang, ang], axis=1).T
    sign = np.where(np.arange(DK) < DK // 2, -1.0, 1.0).astype(np.float32)[:, None]
    cos, sin = np.cos(ang).astype(np.float32), (np.sin(ang).astype(np.float32) * sign).astype(np.float32)
    return np.repeat(cos, NH, axis=0), np.repeat(sin, NH, axis=0)


def kernel(**inputs):
    import concourse.bacc as _bacc
    from concourse.bass_utils import run_bass_kernel_spmd as _run

    nc = _bacc.Bacc("TRN2", target_bir_lowering=False, num_devices=1)
    arrays, args = {}, []
    cos, sin = rope_tables()
    for name, a in [(n, inputs[n]) for n in _INS] + [("rope_cos", cos), ("rope_sin", sin)]:
        a = np.ascontiguousarray(a)
        arrays[f"in_{name}"] = a
        args.append(nc.dram_tensor(f"in_{name}", a.shape, mybir.dt.from_np(a.dtype), kind="ExternalInput").ap())
    args.append(nc.dram_tensor("out_0", (1, S, D), F32, kind="ExternalOutput").ap())
    mixer(nc, *args)
    r = _run(nc, [arrays], core_ids=[0])
    return r.results[0]["out_0"]
```

```python
from contextlib import ExitStack

import numpy as np

import concourse.bass as bass
from concourse import mybir

ALU = mybir.AluOpType
ACT = mybir.ActivationFunctionType
AX = mybir.AxisListType.X
F32 = mybir.dt.float32
F32R = mybir.dt.float32r
BF16 = mybir.dt.bfloat16
U32 = mybir.dt.uint32

P = 128
S = 2048
D = 128
NH = 16
DK = D // NH
HG = 4
NG = NH // HG
NT = S // P
BT = 512
NJ = S // BT
TJ = BT // P
NE = 32
TOPK = 4
NSH = 4
NX = NE + NSH
PIECES = 3
REPS = PIECES
ROWS = PIECES * REPS * DK
MROW = ROWS
SCALE = float(1.0 / np.sqrt(np.float32(DK)))
BIG = 1.0e30
EPS = 1e-5
TWO_ONES = float(np.array([0x3F803F80], np.uint32).view(np.float32)[0])

GROUPS = [(J, G) for J in range(NJ) for G in range(NG)]
STEPS = [(b, J, G, t) for b, (J, G) in enumerate(GROUPS) for t in range(TJ * (J + 1))]
MAXES = [(b, J, G, i, c) for b, (J, G) in enumerate(GROUPS) for i in range(TJ) for c in range(J + 1)]
NSTEP = len(STEPS)
END = [sum(TJ * (J + 1) for J, _ in GROUPS[:b + 1]) for b in range(len(GROUPS))]
NB = len(GROUPS)
LEAD = 21
LAG = 2
NPROB = 3


def plan():
    at = {e: {} for e in ("pe", "act", "dve", "pool", "sp")}
    taken = {}

    def pe(v, task):
        while v in taken:
            v += 1
        taken[v] = task
        at["pe"].setdefault(v, []).append(task)
        return v

    def on(engine, v, *task):
        at[engine].setdefault(v, []).append(task)

    for b in range(NB):
        v = pe(END[b] - LEAD, ("max", b))
        for k in range(5):
            on("dve", v + 1 + k // 3, "max", b, k)
        on("sp", v + 3, "max", b)
    for b in range(NB):
        v = pe(END[b] + LAG, ("out", b))
        on("dve", v + 1, "sums", b)
        on("dve", v + 1, "out", b)

    def prepare(J, v):
        on("dve", v - 6, "stats", J)
        on("dve", v - 5, "aggr", J)
        on("pool", v - 4, "rstd", J)
        on("dve", v - 2, "norm", J)
        v = pe(v, ("xT", J))
        on("act", v + 1, "xT", J)
        v = pe(v + 2, ("q", J))
        on("dve", v + 1, "q", J)
        v = pe(v + 1, ("qf", J))
        on("dve", v + 1, "qf", J)
        on("pool", v + 1, "rope", J, 0)
        v = pe(v + 1, ("k", J))
        on("dve", v + 1, "k", J)
        on("act", v + 2, "p1", J, 0)
        v = pe(v + 1, ("kf", J))
        on("dve", v + 1, "kf", J)
        on("pool", v + 1, "rope", J, 1)
        on("dve", v + 2, "r1", J, 0)
        on("act", v + 3, "p1", J, 1)
        on("act", v + 3, "p2", J, 0)
        on("dve", v + 4, "r1", J, 1)
        on("dve", v + 4, "p3", J, 0)
        on("act", v + 5, "p2", J, 1)
        on("dve", v + 6, "p3", J, 1)
        on("sp", v + 6, "pieces", J)
        w = pe(v + 1, ("v", J))
        on("act", w + 1, "v", J)
        on("sp", max(v + 6, END[4 * J - 5] + LAG + 1 if J >= 2 else v), "stacks", J)
        return v

    def finish(J, v):
        v = pe(v, ("aT", J))
        on("act", v + 1, "aT", J)
        v = pe(v + 2, ("y", J))
        on("dve", v + 1, "y", J)
        on("dve", v + 2, "stats2", J)
        on("dve", v + 3, "aggr2", J)
        on("pool", v + 4, "rstd2", J)
        on("dve", v + 5, "norm2", J)
        v = pe(v + 6, ("xT2", J))
        on("act", v + 1, "xT2", J)
        on("dve", v + 2, "low", J)
        v = pe(v + 2, ("lg", J))
        for k in range(3):
            on("dve", v + 1 + k, "route", J, k)
        on("act", v + 4, "route", J)
        for k in range(3, 17):
            on("dve", v + 5 + (k - 3) // 2, "route", J, k)
        v = pe(v + 13, ("wT", J))
        on("dve", v + 1, "wT", J)
        on("sp", v + 1, "wT", J)

    prepare(0, -60)
    prepare(1, -50)
    prepare(2, -18)
    prepare(3, 18)
    for J in range(NJ):
        finish(J, END[4 * J + 3] + LAG + 2)
    first = min(min(a) for a in at.values())
    last = max(max(a) for a in at.values())
    order = {task: n for n, (v, task) in enumerate(sorted(taken.items()))}
    return at, order, first, last


AT, USE, FIRST, LAST = plan()


def mixer(nc, x_in, wq_in, wk_in, wv_in, wo_in, rw_in, rb_in, gw_in, uw_in, dw_in, sg_in, su_in, sd_in,
          cos_in, sin_in, out):
    with ExitStack() as ctx:
        def sb(name, shape, dt, to=ctx):
            return to.enter_context(nc.sbuf_tensor(name, shape, dt))

        def sem(name):
            return ctx.enter_context(nc.semaphore(name))

        qp_d = nc.dram_tensor("qp_d", [NJ, PIECES, P, BT], BF16).ap()
        kp_d = nc.dram_tensor("kp_d", [NJ, 2 * PIECES - 1, P, BT], BF16).ap()
        zero_d = nc.dram_tensor("zero_d", [PIECES, NH * BT], BF16).ap()
        wt_d = nc.dram_tensor("wt_d", [NX, S], F32).ap()

        xs = sb("xs", [P, NT, D], F32)
        ident = sb("ident", [P, P], F32)
        negI = sb("negI", [P, P], BF16)
        later_k = sb("later_k", [P, P], BF16)
        later_p = sb("later_p", [P, P], BF16)
        iota_e = sb("iota_e", [P, NE], F32)
        iota_i = sb("iota_i", [P, NE], mybir.dt.int32)
        xh = sb("xh", [P, S], F32R)
        xl = sb("xl", [P, S], F32R)
        zb = sb("zb", [P, P], BF16)
        zr = sb("zr", [P, BT], BF16)
        rwT = sb("rwT", [P, NE], F32)
        bias = sb("bias", [P, NE], F32)
        wT = sb("wT", [P, 6, D], F32)

        attn_mem = ExitStack()
        kst = sb("kst", [P, NJ, NH, BT], BF16, attn_mem)
        qst = sb("qst", [P, 2, NH, BT], BF16, attn_mem)
        vext = sb("vext", [P, NT, NH, DK + 1], F32, attn_mem)
        prob = sb("prob", [P, NPROB, HG, BT], F32, attn_mem)
        cos_t = sb("cos_t", [P, BT], F32, attn_mem)
        sin_t = sb("sin_t", [P, BT], F32, attn_mem)
        ccos = sb("ccos", [P, 2, BT], F32, attn_mem)
        csin = sb("csin", [P, 2, BT], F32, attn_mem)
        piece = sb("piece", [P, 2, PIECES, BT], BF16, attn_mem)
        xn = sb("xn", [P, 2, TJ, D], F32, attn_mem)
        xnT = sb("xnT", [P, BT], F32, attn_mem)
        xfT = sb("xfT", [P, BT], F32, attn_mem)
        attn = sb("attn", [P, 2, TJ, D], F32, attn_mem)
        aT = sb("aT", [P, BT], F32, attn_mem)
        ot = sb("ot", [P, BT], F32, attn_mem)
        pmax = sb("pmax", [P, 2, HG, TJ, NJ], F32, attn_mem)
        negm = sb("negm", [P, 2, HG * TJ], F32, attn_mem)
        mrow = sb("mrow", [HG * TJ, 2, P], F32, attn_mem)
        mp = sb("mp", [HG * TJ, PIECES, P], BF16, attn_mem)
        rsum = sb("rsum", [P, TJ, HG], F32, attn_mem)
        half = sb("half", [NSH, BT], F32, attn_mem)
        stats = sb("stats", [P, 2, TJ, 6], F32, attn_mem)
        mv = sb("mv", [P, 2, TJ, 2], F32, attn_mem)
        veps = sb("veps", [P, 2, TJ], F32, attn_mem)
        rstd = sb("rstd", [P, 2, TJ], F32, attn_mem)
        mhalf = sb("mhalf", [P, TJ], F32, attn_mem)
        wnat = prob[:, 0, 0, :].rearrange("p (k d) -> p k d", k=4)
        rwn = prob[0:NE, 0, 1, 0:D]
        lg = sb("lg", [P, TJ, NE], F32, attn_mem)
        ex = sb("ex", [P, TJ, NE], F32, attn_mem)
        sc = sb("sc", [P, TJ, NE], F32, attn_mem)
        mx = sb("mx", [P, TJ], F32, attn_mem)
        sm = sb("sm", [P, TJ], F32, attn_mem)
        rs = sb("rs", [P, TJ], F32, attn_mem)
        top = sb("top", [P, TJ, 8], F32, attn_mem)
        idx = sb("idx", [P, TJ, 8], U32, attn_mem)
        idxf = sb("idxf", [P, TJ, TOPK], F32, attn_mem)
        ts4 = sb("ts4", [P, TJ], F32, attn_mem)
        tc4 = sb("tc4", [P, TJ], F32, attn_mem)
        tr4 = sb("tr4", [P, TJ], F32, attn_mem)
        w4 = sb("w4", [P, TJ, TOPK], F32, attn_mem)
        hot = sb("hot", [P, TJ, TOPK, NE], F32, attn_mem)
        wtok = sb("wtok", [P, TJ, NE], F32, attn_mem)
        wTs = sb("wTs", [NE, BT], F32, attn_mem)
        attn_mem.close()

        ewn = sb("ewn", [P, 2, 3, D], F32)
        ehi = sb("ehi", [P, 2, 2, D], F32R)
        elo = sb("elo", [P, 2, 2, D], F32R)
        edn = sb("edn", [P, 2, D], F32)
        wrow = sb("wrow", [1, 2, S], F32)
        wb = sb("wb", [P, 2, S], F32)
        th = sb("th", [P, 2, BT], F32)
        ga = sb("ga", [P, 2, BT], F32)
        hh = sb("hh", [P, 2, BT], F32)
        hw = sb("hw", [P, NJ, BT], F32)
        fin = sb("fin", [P, NJ, BT], F32)
        yo = sb("yo", [P, NT, D], F32)

        bank = [ctx.enter_context(nc.psum_tensor(f"bank{i}", [P, 512], F32)) for i in range(2)]
        pair = [ctx.enter_context(nc.psum_tensor(f"pair{i}", [P, 2, 512], F32)) for i in range(2)]
        accb = ctx.enter_context(nc.psum_tensor("accb", [P, 512], F32))
        misc = ctx.enter_context(nc.psum_tensor("misc", [P, 512], F32))

        names = """w_in rw_in c_mem c_done stk_mem vc_z z_store half_m half_st misc_pe misc_read wt_pe wt_act rwt_pe rwt_dve
            st_done ag_done ve_done rstd_done xn_done xt_act rp_cos rp_sin rp_add rp_p1 rp_r1 rp_p2 rp_p3 v_act
            mm_pe mx_rd mx_fin ms_part ms_dve m_row qk_pe ex_act av_pe ot_act rs_out at_done acc_z
            a_act x2_dve st2 ag2 ve2 rstd2 xn2 xh_act low_dve r_dve r_act wt_dve w_st
            et_pe eh_act el_dve gu_pe th_act ga_dve hh_dve hw_pool wb_pool dn_pe ew_z fin_act ft_pe yo_dve o_st acc0""".split()
        s = {n: sem(n) for n in names}
        x_in_s = [sem(f"x_in{J}") for J in range(NJ)]
        tab_in = [sem(f"tab_in{J}") for J in range(NJ)]
        p_store = [sem(f"p_store{J}") for J in range(NJ)]
        stk_in = [sem(f"stk_in{J}") for J in range(NJ)]
        ew_in = [sem(f"ew_in{k}") for k in range(2)]
        wr_in = [sem(f"wr_in{k}") for k in range(2)]

        block = ctx.enter_context(nc.Block())
        PER = HG
        LOADS = 2 * REPS + 1

        def tok(J):
            return slice(J * BT, (J + 1) * BT)

        def tasks(engine, v):
            return AT[engine].get(v, [])

        @block.sync
        def _(sp):
            for J in range(NJ):
                sp.dma_start(xs[:, J * TJ:(J + 1) * TJ, :],
                             x_in[0, tok(J), :].rearrange("(t p) d -> p t d", p=P)).then_inc(x_in_s[J], 16)
                if J == 0:
                    sp.dma_start(cos_t[:], cos_in[:, tok(J)]).then_inc(tab_in[J], 16)
                    sp.dma_start(sin_t[:], sin_in[:, tok(J)]).then_inc(tab_in[J], 16)
            sp.wait_ge(s["stk_mem"], 2)
            sp.dma_start(zero_d, qst[96:96 + PIECES, 0].rearrange("p h s -> p (h s)")).then_inc(s["z_store"], 16)
            sp.wait_ge(s["half_m"], 1)
            for J in range(NJ):
                sp.dma_start(wt_d[0:NSH, tok(J)], half[:]).then_inc(s["half_st"], 16)

            def pieces(J):
                for side, dst in ((0, qp_d), (1, kp_d)):
                    sp.wait_ge(s["rp_p3"], 2 * J + side + 1)
                    sp.dma_start(dst[J, 0:PIECES].rearrange("c p s -> p c s"), piece[:, side, :, :])\
                        .then_inc(p_store[J], 16)
                sp.dma_start(kp_d[J, PIECES:].rearrange("c p s -> p c s"), piece[:, 1, 0:PIECES - 1, :])\
                    .then_inc(p_store[J], 16)
                if J + 1 < NJ:
                    sp.dma_start(cos_t[:], cos_in[:, tok(J + 1)]).then_inc(tab_in[J + 1], 16)
                    sp.dma_start(sin_t[:], sin_in[:, tok(J + 1)]).then_inc(tab_in[J + 1], 16)

            def stacks(J):
                sp.wait_ge(p_store[J], 16 * 3)
                sp.wait_ge(s["z_store"], 16)
                sp.wait_ge(s["stk_mem"], 2 + NJ)
                if J >= 2:
                    sp.wait_ge(s["av_pe"], END[4 * J - 5])
                for r in range(REPS):
                    rows = slice(r * PIECES * DK, (r + 1) * PIECES * DK)
                    sp.dma_start(kst[rows, J].rearrange("q h s -> q (h s)"),
                                 kp_d[J, r:r + PIECES].rearrange("c (r h) s -> (c r) (h s)", h=NH)).then_inc(stk_in[J], 16)
                    sp.dma_start(qst[rows, J % 2].rearrange("q h s -> q (h s)"),
                                 qp_d[J].rearrange("c (r h) s -> (c r) (h s)", h=NH)).then_inc(stk_in[J], 16)
                sp.dma_start(qst[MROW:MROW + PIECES, J % 2].rearrange("p h s -> p (h s)"), zero_d).then_inc(stk_in[J], 16)

            def store_m(b):
                J, G = GROUPS[b]
                sp.wait_ge(s["ms_dve"], b + 1)
                for c in range(PIECES):
                    sp.dma_start(qst[MROW + c:MROW + c + 1, J % 2, G * HG:(G + 1) * HG].rearrange("c h s -> c (h s)"),
                                 mp[:, c, :]).then_inc(s["m_row"], 16)

            def store_w(J):
                sp.wait_ge(s["wt_dve"], J + 1)
                sp.dma_start(wt_d[NSH:, tok(J)], wTs[:]).then_inc(s["w_st"], 16)

            for v in range(FIRST, LAST + 1):
                for task, *a in tasks("sp", v):
                    {"pieces": pieces, "stacks": stacks, "max": store_m, "wT": store_w}[task](*a)

            def expert_weights(buf, g, u, d):
                for k, w in enumerate((g, u, d)):
                    sp.dma_start(ewn[:, buf, k, :], w).then_inc(ew_in[buf], 16)

            def row(buf, w):
                sp.dma_start(wrow[:, buf, :], w).then_inc(wr_in[buf], 16)

            sp.wait_ge(s["at_done"], NG * NJ)
            sp.wait_ge(s["half_st"], 16 * NJ)
            for c in range(NSH):
                if c >= 2:
                    sp.wait_ge(s["et_pe"], c - 1)
                    sp.wait_ge(s["wb_pool"], c - 1)
                h = slice(c * D, (c + 1) * D)
                expert_weights(c % 2, sg_in[h, :], su_in[h, :], sd_in[:, h])
                row(c % 2, wt_d[c:c + 1, :])
            sp.wait_ge(s["w_st"], 16 * NJ)
            with sp.Fori(0, NE // 2) as i:
                for k in range(2):
                    e = 2 * i
                    sp.wait_ge(s["et_pe"], e + (NSH + k - 1))
                    sp.wait_ge(s["wb_pool"], e + (NSH + k - 1))
                    one = bass.ds(e + k, 1)
                    expert_weights(k, *(w[one, :, :].rearrange("a p d -> (a p) d") for w in (gw_in, uw_in, dw_in)))
                    row(k, wt_d[bass.ds(e + (NSH + k), 1), :])
            sp.wait_ge(s["et_pe"], NX - 1)
            sp.wait_ge(s["wb_pool"], NX - 1)
            expert_weights(0, gw_in[0], uw_in[0], dw_in[0])
            row(0, wt_d[0:1, :])
            for J in range(NJ):
                sp.wait_ge(s["yo_dve"], J + 1)
                sp.dma_start(out[0, tok(J), :].rearrange("(t p) d -> p t d", p=P),
                             yo[:, J * TJ:(J + 1) * TJ, :]).then_inc(s["o_st"], 16)
            sp.wait_ge(s["o_st"], 16 * NJ)

        @block.gpsimd
        def _(pool):
            pool.memset(ident[:], 0.0).then_inc(s["c_mem"], 1)
            pool.memset(negI[:], 0.0).then_inc(s["c_mem"], 1)
            pool.memset(later_k[:], 1.0).then_inc(s["c_mem"], 1)
            pool.memset(later_p[:], 1.0).then_inc(s["c_mem"], 1)
            pool.wait_ge(s["c_mem"], 4)
            pool.affine_select(out=ident[:], in_=ident[:], compare_op=ALU.not_equal, fill=1.0, base=0,
                               pattern=[[-1, P]], channel_multiplier=1).then_inc(s["c_done"], 1)
            pool.affine_select(out=negI[:], in_=negI[:], compare_op=ALU.not_equal, fill=-BIG, base=0,
                               pattern=[[-1, P]], channel_multiplier=1).then_inc(s["c_done"], 1)
            pool.affine_select(out=later_k[:], in_=later_k[:], compare_op=ALU.is_gt, fill=0.0, base=0,
                               pattern=[[1, P]], channel_multiplier=-1).then_inc(s["c_done"], 1)
            pool.affine_select(out=later_p[:], in_=later_p[:], compare_op=ALU.is_gt, fill=0.0, base=0,
                               pattern=[[-1, P]], channel_multiplier=1).then_inc(s["c_done"], 1)
            pool.iota(iota_i[:], pattern=[[1, NE]], base=0, channel_multiplier=0).then_inc(s["c_done"], 1)
            pool.memset(half[:], 0.5).then_inc(s["half_m"], 1)
            pool.memset(mhalf[:], -0.5).then_inc(s["half_m"], 1)
            pool.wait_ge(s["c_done"], 5)
            pool.wait_ge(s["half_m"], 2)

            def rstd_of(ag, ve, done, which, J):
                pool.wait_ge(s[ag], TJ * (J + 1))
                pool.tensor_scalar(veps[:, which, :], mv[:, which, :, 1], EPS, 0.0, ALU.add, ALU.add).then_inc(s[ve], 1)
                pool.wait_ge(s[ve], J + 1)
                pool.tensor_tensor(rstd[:, which, :], veps[:, which, :], mhalf[:], ALU.pow).then_inc(s[done], 1)

            def rope(J, side):
                pool.wait_ge(s["rp_sin"], 2 * J + side + 1)
                pool.tensor_tensor(ccos[:, side, :], ccos[:, side, :], csin[:, side, :], ALU.add).then_inc(s["rp_add"], 1)

            def pool_tasks(v):
                for task, *a in tasks("pool", v):
                    if task == "rstd":
                        rstd_of("ag_done", "ve_done", "rstd_done", 0, *a)
                    elif task == "rstd2":
                        rstd_of("ag2", "ve2", "rstd2", 1, *a)
                    else:
                        rope(*a)

            for v in range(FIRST, -60):
                pool_tasks(v)
            pool.wait_ge(s["rstd_done"], 1)
            for par in range(2):
                pool.memset(qst[64:P, par].rearrange("p h s -> p (h s)").bitcast(F32), 0.0).then_inc(s["stk_mem"], 1)
            for J in range(NJ):
                pool.memset(kst[64:P, J].rearrange("p h s -> p (h s)").bitcast(F32), TWO_ONES).then_inc(s["stk_mem"], 1)
            pool.wait_ge(s["stk_mem"], 2 + NJ)
            pool.memset(vext[:, :, :, DK:DK + 1], 1.0).then_inc(s["vc_z"], 1)
            pool.memset(zb[:], 0.0).then_inc(s["ew_z"], 1)
            pool.memset(zr[:], 0.0).then_inc(s["ew_z"], 1)
            for v in range(-60, LAST + 1):
                pool_tasks(v)

            pool.wait_ge(s["wt_dve"], NJ)
            pool.memset(edn[:, 1, :], 0.0).then_inc(s["ew_z"], 1)
            for J in (NJ - 2, NJ - 1):
                pool.memset(hw[:, J, :], 0.0).then_inc(s["hw_pool"], 1)

            def row_ready(i, e, buf):
                pool.wait_ge(wr_in[buf], 16 * i + 16)
                pool.wait_ge(s["hw_pool"], e * NJ - 2)

            def spread(buf):
                pool.partition_broadcast(wb[:, buf, :], wrow[:, buf, :]).then_inc(s["wb_pool"], 1)

            def weigh(e, buf, J):
                n = e * NJ + J
                pool.wait_ge(s["hh_dve"], n + 3)
                if J == 0:
                    pool.wait_ge(s["wb_pool"], e + 1)
                pool.wait_ge(s["dn_pe"], n + 1)
                pool.tensor_tensor(hw[:, J, :], hh[:, J % 2, :], wb[:, buf, tok(J)], ALU.mult)\
                    .then_inc(s["hw_pool"], 1)

            pool.wait_ge(wr_in[0], 16)
            pool.partition_broadcast(wb[:, 0, :], wrow[:, 0, :]).then_inc(s["wb_pool"], 1)
            with pool.Fori(0, NX // 2) as i:
                for k in range(2):
                    weigh(2 * i + k, k, 0)
                    row_ready(i + k, 2 * i + (k + 1), 1 - k)
                    weigh(2 * i + k, k, 1)
                    spread(1 - k)
                    weigh(2 * i + k, k, 2)
                    weigh(2 * i + k, k, 3)

        @block.scalar
        def _(act):
            for k, w in enumerate((wq_in, wk_in, wv_in, wo_in)):
                act.dma_start(wnat[:, k, :], w).then_inc(s["w_in"], 16)
            act.dma_start(rwn, rw_in).then_inc(s["rw_in"], 16)
            act.dma_start(bias[:], rb_in.rearrange("(a e) -> a e", a=1).to_broadcast([P, NE])).then_inc(s["rw_in"], 16)

            act.wait_ge(s["wt_pe"], 4)
            for k in range(2):
                src = bank[1][:, k * D:(k + 1) * D]
                act.activation(wT[:, 2 * k, :].rearrange("p (r h) -> p h r", h=NH),
                               src.rearrange("p (h r) -> p h r", h=NH), ACT.Copy).then_inc(s["wt_act"], 1)
                for a in range(2):
                    act.activation(wT[:, 2 * k + 1, a * (D // 2):(a + 1) * (D // 2)].rearrange("p (r h) -> p h r", h=NH),
                                   src.rearrange("p (h a r) -> p h a r", h=NH, a=2)[:, :, 1 - a, :], ACT.Copy)\
                        .then_inc(s["wt_act"], 1)
            act.activation(wT[:, 4:6, :].rearrange("p a d -> p (a d)"), bank[1][:, 2 * D:4 * D], ACT.Copy)\
                .then_inc(s["wt_act"], 1)

            def act_exp(u, p):
                b, J, G, t = STEPS[u]
                c0 = max(t - TJ * J, 0) * P
                act.wait_ge(s["qk_pe"], 2 * u + p + 1)
                if u >= NPROB:
                    act.wait_ge(s["av_pe"], u - NPROB + 1)
                act.activation(prob[:, u % NPROB, 2 * p:2 * p + 2, c0:], pair[p][:, :, c0:], ACT.Exp, scale=SCALE)\
                    .then_inc(s["ex_act"], 1)

            def act_sums(b):
                act.wait_ge(s["av_pe"], END[b])
                if b:
                    act.wait_ge(s["misc_pe"], USE[("out", b - 1)] + 1)
                act.activation(ot[:], accb[:], ACT.Copy).then_inc(s["ot_act"], 1)

            def act_task(task, J, *a):
                if task in ("xT", "v", "aT", "xT2"):
                    act.wait_ge(s["misc_pe"], USE[(task, J)] + 1)
                if task == "xT":
                    act.activation(xnT[:], misc[:], ACT.Copy).then_inc(s["misc_read"], 1)
                elif task == "v":
                    act.activation(vext[:, J * TJ:(J + 1) * TJ, :, 0:DK],
                                   misc[:].rearrange("p (t h r) -> p t h r", t=TJ, h=NH), ACT.Copy)\
                        .then_inc(s["misc_read"], 1)
                elif task == "aT":
                    act.activation(aT[:], misc[:], ACT.Copy).then_inc(s["misc_read"], 1)
                elif task == "xT2":
                    act.activation(xfT[:], misc[:], ACT.Copy).then_inc(s["misc_read"], 1)
                    act.wait_ge(s["misc_read"], USE[(task, J)] + 1)
                    act.activation(xh[:, tok(J)], xfT[:], ACT.Copy).then_inc(s["xh_act"], 1)
                elif task == "p1":
                    side, = a
                    act.wait_ge(s["rp_add"], 2 * J + side + 1)
                    if J:
                        act.wait_ge(p_store[J - 1], 16 * 3)
                    act.activation(piece[:, side, 0, :], ccos[:, side, :], ACT.Copy).then_inc(s["rp_p1"], 1)
                elif task == "p2":
                    side, = a
                    act.wait_ge(s["rp_r1"], 2 * J + side + 1)
                    act.activation(piece[:, side, 1, :], csin[:, side, :], ACT.Copy).then_inc(s["rp_p2"], 1)
                elif task == "route":
                    act.wait_ge(s["r_dve"], 17 * J + 3)
                    act.activation(ex[:], sc[:], ACT.Exp).then_inc(s["r_act"], 1)

            act.wait_ge(s["vc_z"], 1)
            for v in range(FIRST, LAST + 1):
                if 0 <= v < NSTEP:
                    act_exp(v, 0)
                for b in range(NB):
                    if v == END[b] - 1 + LAG:
                        act_sums(b)
                for task, *a in tasks("act", v):
                    act_task(task, *a)
                if 0 <= v < NSTEP:
                    act_exp(v, 1)

            def turned_weights(e, buf, slot):
                act.wait_ge(s["et_pe"], e + 1)
                act.activation(ehi[:, buf, :, :].rearrange("p a d -> p (a d)"), pair[slot][:, 0, 0:2 * D], ACT.Copy)\
                    .then_inc(s["eh_act"], 1)
                act.activation(edn[:, buf, :], pair[slot][:, 1, 0:D], ACT.Copy).then_inc(s["eh_act"], 1)

            def gate(e, J, slot):
                n = e * NJ + J
                act.wait_ge(s["gu_pe"], n + 1)
                act.wait_ge(s["ga_dve"], n + 1)
                act.activation(th[:, J % 2, :], pair[slot][:, 0, :], ACT.Tanh, scale=0.5).then_inc(s["th_act"], 1)

            act.wait_ge(s["ew_z"], 3)
            turned_weights(0, 0, 1)
            with act.Fori(0, NX // 2) as i:
                for k in range(2):
                    e = 2 * i
                    gate(e + k, 0, k)
                    gate(e + k, 1, 1 - k)
                    gate(e + k, 2, k)
                    turned_weights(e + (k + 1), 1 - k, 1 - k)
                    gate(e + k, 3, k)
            for J in range(NJ):
                act.wait_ge(s["acc0"], 1)
                act.activation(fin[:, J, :], [accb, misc, bank[0], bank[1]][J][:], ACT.Copy).then_inc(s["fin_act"], 1)

        @block.tensor
        def _(pe):
            def mm(out, a, b, start=True, stop=True, loose=False):
                return nc.tensor.matmul(out, a, b, start=start, stop=stop, skip_group_check=loose)

            pe.wait_ge(s["c_done"], 5)
            pe.wait_ge(s["w_in"], 16 * 4)
            for k in range(4):
                nc.tensor.transpose(bank[1][:, k * D:(k + 1) * D], wnat[:, k, :], ident[:]).then_inc(s["wt_pe"], 1)
            pe.wait_ge(s["rw_in"], 32)
            nc.tensor.transpose(bank[0][:, 0:NE], rwn, ident[0:NE, 0:NE]).then_inc(s["rwt_pe"], 1)
            pe.wait_ge(s["wt_act"], 7)
            pe.wait_ge(s["rwt_dve"], 1)

            def pe_max(q, h):
                b, J, G, i, c = MAXES[q]
                n = (i + 1) * P if c == J else BT
                if q == 0 or MAXES[q - 1][1] != J:
                    pe.wait_ge(stk_in[J], 16 * LOADS)
                k = HG * q + h
                if k >= 2:
                    pe.wait_ge(s["mx_rd"], k - 1)
                last = mm(bank[h % 2][:, 0:n], qst[:, J % 2, G * HG + h, i * P:(i + 1) * P],
                          kst[:, c, G * HG + h, 0:n], stop=c != J)
                if c == J:
                    last = mm(bank[h % 2][:, i * P:n], negI[:], later_k[:], start=False)
                last.then_inc(s["mm_pe"], 1)

            def pe_scores(u, p):
                b, J, G, t = STEPS[u]
                d = t - TJ * J
                c0 = max(d, 0) * P
                if t == 0:
                    pe.wait_ge(s["m_row"], 16 * PIECES * (b + 1))
                k = 2 * u + p
                if k >= 2:
                    pe.wait_ge(s["ex_act"], k - 1)
                for h in range(2):
                    head = G * HG + 2 * p + h
                    last = mm(pair[p][:, h, c0:], kst[:, t // TJ, head, t % TJ * P:(t % TJ + 1) * P],
                              qst[:, J % 2, head, c0:], stop=d < 0)
                    if d >= 0:
                        last = mm(pair[p][:, h, c0:c0 + P], negI[:], later_p[:], start=False)
                last.then_inc(s["qk_pe"], 1)

            def pe_av(u):
                b, J, G, t = STEPS[u]
                c0 = max(t - TJ * J, 0) * P
                pe.wait_ge(s["ex_act"], 2 * u + 2)
                if t == 0 and b:
                    pe.wait_ge(s["ot_act"], b)
                for h in range(HG):
                    last = mm(accb[32 * h:32 * h + DK + 1, c0:], vext[:, t, G * HG + h, :], prob[:, u % NPROB, h, c0:],
                              start=t == 0, stop=t == TJ * (J + 1) - 1)
                last.then_inc(s["av_pe"], 1)

            def pe_task(task, n):
                use = USE[(task, n)]
                if use:
                    pe.wait_ge(s["misc_read"], use)
                if task == "max":
                    pe.wait_ge(s["mx_fin"], n + 1)
                    last = nc.tensor.transpose(misc[0:HG * TJ, 0:P], negm[:, n % 2, :], ident[:])
                elif task == "out":
                    pe.wait_ge(s["ot_act"], n + 1)
                    for i in range(TJ):
                        last = nc.tensor.transpose(misc[:, i * P:(i + 1) * P], ot[:, i * P:(i + 1) * P], ident[:])
                elif task in ("xT", "xT2"):
                    pe.wait_ge(s["xn_done" if task == "xT" else "xn2"], n + 1)
                    for i in range(TJ):
                        last = nc.tensor.transpose(misc[:, i * P:(i + 1) * P], xn[:, task == "xT2", i, :], ident[:])
                elif task in ("q", "qf", "k", "kf"):
                    last = mm(misc[:], wT[:, ("q", "qf", "k", "kf").index(task), :], xnT[:])
                elif task == "v":
                    for i in range(TJ):
                        last = mm(misc[:, i * P:(i + 1) * P], xnT[:, i * P:(i + 1) * P], wT[:, 4, :])
                elif task == "aT":
                    pe.wait_ge(s["at_done"], NG * (n + 1))
                    for i in range(TJ):
                        last = nc.tensor.transpose(misc[:, i * P:(i + 1) * P], attn[:, n % 2, i, :], ident[:])
                elif task == "y":
                    for i in range(TJ):
                        last = mm(misc[:, i * P:(i + 1) * P], aT[:, i * P:(i + 1) * P], wT[:, 5, :])
                elif task == "lg":
                    for i in range(TJ):
                        last = mm(misc[:, i * NE:(i + 1) * NE], xfT[:, i * P:(i + 1) * P], rwT[:])
                elif task == "wT":
                    pe.wait_ge(s["r_dve"], 17 * (n + 1))
                    for i in range(TJ):
                        last = nc.tensor.transpose(misc[0:NE, i * P:(i + 1) * P], wtok[:, i, :], ident[:])
                last.then_inc(s["misc_pe"], 1)

            pe.wait_ge(s["ew_z"], 2)
            mm(accb[:], zb[:], zr[:])
            for v in range(FIRST, LAST + 1):
                q = v + LEAD
                exps = 0 <= v < NSTEP
                if 0 <= q < NSTEP:
                    pe_max(q, 0)
                if LAG <= v < NSTEP + LAG:
                    pe_av(v - LAG)
                if 0 <= q < NSTEP:
                    pe_max(q, 1)
                if exps:
                    pe_scores(v, 0)
                if 0 <= q < NSTEP:
                    pe_max(q, 2)
                if exps:
                    pe_scores(v, 1)
                if 0 <= q < NSTEP:
                    pe_max(q, 3)
                for task, n in tasks("pe", v):
                    pe_task(task, n)

            out_bank = [accb, misc, bank[0], bank[1]]
            pe.wait_ge(s["wt_dve"], NJ)
            pe.wait_ge(s["low_dve"], NJ)
            pe.wait_ge(s["mx_rd"], HG * NSTEP)
            pe.wait_ge(s["ew_z"], 3)
            for J in range(NJ):
                last = mm(out_bank[J][:], zb[:], zr[:], stop=False, loose=True)
                if J < 2:
                    last.then_inc(s["dn_pe"], 1)

            def turn(i, buf, slot):
                pe.wait_ge(ew_in[buf], 48 * i + 48)
                for k in range(3):
                    last = nc.tensor.transpose(pair[slot][:, k // 2, (k % 2) * D:(k % 2 + 1) * D], ewn[:, buf, k, :], ident[:])
                last.then_inc(s["et_pe"], 1)

            def gate_up(e, buf, J, slot):
                n = e * NJ + J
                if J == 0:
                    pe.wait_ge(s["eh_act"], 2 * e + 2)
                    pe.wait_ge(s["el_dve"], e + 1)
                for k in range(2):
                    o = pair[slot][:, k, :]
                    mm(o, ehi[:, buf, k, :], xh[:, tok(J)], stop=False)
                    mm(o, ehi[:, buf, k, :], xl[:, tok(J)], start=False, stop=False)
                    last = mm(o, elo[:, buf, k, :], xh[:, tok(J)], start=False)
                last.then_inc(s["gu_pe"], 1)

            def down(n, buf, J):
                pe.wait_ge(s["hw_pool"], n + 1)
                mm(out_bank[J][:], edn[:, buf, :], hw[:, J, :], start=False, stop=False, loose=True)\
                    .then_inc(s["dn_pe"], 1)

            turn(0, 0, 1)
            with pe.Fori(0, NX // 2) as i:
                for k in range(2):
                    e = 2 * i + k
                    n = e * NJ
                    gate_up(e, k, 0, k)
                    down(n, 1 - k, NJ - 2)
                    pe.wait_ge(s["hh_dve"], n + 2)
                    gate_up(e, k, 1, 1 - k)
                    down(n + 1, 1 - k, NJ - 1)
                    pe.wait_ge(s["hh_dve"], n + 3)
                    gate_up(e, k, 2, k)
                    down(n + 2, k, 0)
                    pe.wait_ge(s["hh_dve"], n + 4)
                    turn(i + k, 1 - k, 1 - k)
                    pe.wait_ge(s["hh_dve"], n + 5)
                    gate_up(e, k, 3, k)
                    down(n + 3, k, 1)
            for J in (NJ - 2, NJ - 1):
                down(NX * NJ + J - (NJ - 2), 1, J)
            for J in range(NJ):
                last = mm(out_bank[J][:], zb[:], zr[:], start=False, loose=True)
            last.then_inc(s["acc0"], 1)
            pe.wait_ge(s["eh_act"], 2 * (NX + 1))
            pe.wait_ge(s["el_dve"], NX + 1)
            for J in range(NJ):
                pe.wait_ge(s["fin_act"], J + 1)
                for i in range(TJ):
                    last = nc.tensor.transpose(pair[J // 2][:, J % 2, i * P:(i + 1) * P], fin[:, J, i * P:(i + 1) * P], ident[:])
                last.then_inc(s["ft_pe"], 1)

        @block.vector
        def _(dve):
            dve.wait_ge(s["rwt_pe"], 1)
            dve.tensor_copy(rwT[:], bank[0][:, 0:NE]).then_inc(s["rwt_dve"], 1)
            dve.wait_ge(s["c_done"], 5)
            dve.tensor_copy(iota_e[:], iota_i[:]).then_inc(s["rwt_dve"], 1)

            def dve_max(q, h):
                b, J, G, i, c = MAXES[q]
                n = (i + 1) * P if c == J else BT
                if h == 0 and i == 0 and c == 0 and b >= 2:
                    dve.wait_ge(s["mx_fin"], b - 1)
                dve.wait_ge(s["mm_pe"], HG * q + h + 1)
                dve.tensor_reduce(pmax[:, b % 2, h, i, c:c + 1], bank[h % 2][:, 0:n], AX, ALU.max).then_inc(s["mx_rd"], 1)

            def last_max(b):
                J, G = GROUPS[b]
                dve.wait_ge(s["mx_rd"], HG * END[b])
                if b >= 2:
                    dve.wait_ge(s["misc_pe"], USE[("max", b - 2)] + 1)
                dve.tensor_reduce(negm[:, b % 2, :], pmax[:, b % 2, :, :, 0:J + 1].rearrange("p h i c -> p (h i) c"), AX,
                                  ALU.max, negate=True).then_inc(s["mx_fin"], 1)

            def split_max(b, k):
                if k == 0:
                    dve.wait_ge(s["misc_pe"], USE[("max", b)] + 1)
                    dve.tensor_copy(mrow[:, 0, :], misc[0:HG * TJ, 0:P]).then_inc(s["misc_read"], 1)
                elif k == 1:
                    dve.wait_ge(s["misc_read"], USE[("max", b)] + 1)
                    if b:
                        dve.wait_ge(s["m_row"], 16 * PIECES * b)
                    dve.tensor_copy(mp[:, 0, :], mrow[:, 0, :]).then_inc(s["ms_part"], 1)
                elif k == 2:
                    dve.wait_ge(s["ms_part"], 3 * b + 1)
                    dve.tensor_tensor(mrow[:, 1, :], mrow[:, 0, :], mp[:, 0, :], ALU.subtract).then_inc(s["ms_part"], 1)
                elif k == 3:
                    dve.wait_ge(s["ms_part"], 3 * b + 2)
                    dve.tensor_copy(mp[:, 1, :], mrow[:, 1, :]).then_inc(s["ms_part"], 1)
                else:
                    dve.wait_ge(s["ms_part"], 3 * b + 3)
                    dve.tensor_tensor(mp[:, 2, :], mrow[:, 1, :], mp[:, 1, :], ALU.subtract).then_inc(s["ms_dve"], 1)

            rows = misc[:].rearrange("p (i h r) -> p i h r", i=TJ, h=HG)

            def out_sums(b):
                dve.wait_ge(s["misc_pe"], USE[("out", b)] + 1)
                if b:
                    dve.wait_ge(s["at_done"], b)
                dve.reciprocal(rsum[:], rows[:, :, :, DK]).then_inc(s["rs_out"], 1)

            def out_scaled(b):
                J, G = GROUPS[b]
                dve.wait_ge(s["rs_out"], b + 1)
                if J >= 2 and G == 0:
                    dve.wait_ge(s["misc_pe"], USE[("aT", J - 2)] + 1)
                dst = attn[:, J % 2].rearrange("p i (g h r) -> p i g h r", g=NG, h=HG)
                dve.tensor_tensor(dst[:, :, G], rows[:, :, :, 0:DK], rsum[:].unsqueeze(3).to_broadcast([P, TJ, HG, DK]),
                                  ALU.mult).then_inc(s["at_done"], 1)
                dve.wait_ge(s["at_done"], b + 1)
                dve.sem_inc(s["misc_read"], 1)

            def statistics(st, which, J):
                for i in range(TJ):
                    last = dve.bn_stats(stats[:, which, i, :], xs[:, J * TJ + i, :])
                last.then_inc(s[st], 1)

            def aggregate(st, ag, done, which, J):
                dve.wait_ge(s[st], J + 1)
                if J:
                    dve.wait_ge(s[done], J)
                for i in range(TJ):
                    dve.bn_aggr(mv[:, which, i, :], stats[:, which, i, :]).then_inc(s[ag], 1)

            def normalise(rst, done, task, which, J):
                dve.wait_ge(s[rst], J + 1)
                if J:
                    dve.wait_ge(s["misc_pe"], USE[(task, J - 1)] + 1)
                for i in range(TJ):
                    last = dve.tensor_scalar(xn[:, which, i, :], xs[:, J * TJ + i, :], mv[:, which, i, 0:1],
                                             rstd[:, which, i:i + 1], ALU.subtract, ALU.mult)
                last.then_inc(s[done], 1)

            def rope_product(task, J):
                side, flip = ("q", "qf", "k", "kf").index(task) // 2, task[1:] == "f"
                table, dst = (sin_t, csin) if flip else (cos_t, ccos)
                dve.wait_ge(s["misc_pe"], USE[(task, J)] + 1)
                if task == "q":
                    dve.wait_ge(tab_in[J], 32)
                if J:
                    dve.wait_ge(s["rp_r1"], 2 * (J - 1) + side + 1)
                    dve.wait_ge(s["rp_p3"], 2 * (J - 1) + side + 1)
                    dve.wait_ge(s["rp_p2"], 2 * (J - 1) + side + 1)
                dve.tensor_tensor(dst[:, side, :], misc[:], table[:], ALU.mult)\
                    .then_inc(s["misc_read"], 1)
                if flip:
                    dve.wait_ge(s["misc_read"], USE[(task, J)] + 1)
                    dve.sem_inc(s["rp_sin"], 1)

            def rest(J, side):
                dve.wait_ge(s["rp_p1"], 2 * J + side + 1)
                dve.tensor_tensor(csin[:, side, :], ccos[:, side, :], piece[:, side, 0, :], ALU.subtract)\
                    .then_inc(s["rp_r1"], 1)

            def third(J, side):
                dve.wait_ge(s["rp_p2"], 2 * J + side + 1)
                dve.tensor_tensor(piece[:, side, 2, :], csin[:, side, :], piece[:, side, 1, :], ALU.subtract)\
                    .then_inc(s["rp_p3"], 1)

            def residual(J):
                dve.wait_ge(s["misc_pe"], USE[("y", J)] + 1)
                cols = slice(J * TJ, (J + 1) * TJ)
                dve.tensor_tensor(xs[:, cols, :], xs[:, cols, :], misc[:].rearrange("p (i d) -> p i d", i=TJ), ALU.add)\
                    .then_inc(s["misc_read"], 1)

            def low(J):
                dve.wait_ge(s["xh_act"], J + 1)
                dve.tensor_tensor(xl[:, tok(J)], xfT[:], xh[:, tok(J)].bitcast(F32), ALU.subtract).then_inc(s["low_dve"], 1)

            def route(J, k):
                full, wide = [P, TJ, NE], [P, TJ, TOPK, NE]
                if k == 0:
                    dve.wait_ge(s["misc_pe"], USE[("lg", J)] + 1)
                    dve.wait_ge(s["rw_in"], 32)
                if 17 * J + k:
                    dve.wait_ge(s["r_dve"], 17 * J + k)
                if k == 3:
                    dve.wait_ge(s["r_act"], J + 1)
                if k == 16 and J:
                    dve.wait_ge(s["misc_pe"], USE[("wT", J - 1)] + 1)
                if k == 0:
                    last = dve.tensor_tensor(lg[:], misc[:, 0:TJ * NE].rearrange("p (t e) -> p t e", t=TJ),
                                             bias[:].unsqueeze(1).to_broadcast(full), ALU.add)
                elif k == 1:
                    last = dve.tensor_reduce(mx[:], lg[:], AX, ALU.max)
                elif k == 2:
                    last = dve.tensor_tensor(sc[:], lg[:], mx[:].unsqueeze(2).to_broadcast(full), ALU.subtract)
                elif k == 3:
                    last = dve.tensor_reduce(sm[:], ex[:], AX, ALU.add)
                elif k == 4:
                    last = dve.reciprocal(rs[:], sm[:])
                elif k == 5:
                    last = dve.tensor_tensor(lg[:], ex[:], rs[:].unsqueeze(2).to_broadcast(full), ALU.mult)
                elif k == 6:
                    for t in range(TJ):
                        last = dve.max(top[:, t, :], lg[:, t, :])
                elif k == 7:
                    for t in range(TJ):
                        last = dve.max_index(idx[:, t, :], top[:, t, :], lg[:, t, :])
                elif k == 8:
                    last = dve.tensor_copy(idxf[:], idx[:, :, 0:TOPK])
                elif k == 9:
                    last = dve.tensor_reduce(ts4[:], top[:, :, 0:TOPK], AX, ALU.add)
                elif k == 10:
                    last = dve.tensor_scalar(tc4[:], ts4[:], 1e-12, 2.0, ALU.max, ALU.mult)
                elif k == 11:
                    last = dve.reciprocal(tr4[:], tc4[:])
                elif k == 12:
                    last = dve.tensor_tensor(w4[:], top[:, :, 0:TOPK], tr4[:].unsqueeze(2).to_broadcast([P, TJ, TOPK]), ALU.mult)
                elif k == 13:
                    last = dve.tensor_tensor(hot[:], iota_e[:].unsqueeze(1).unsqueeze(1).to_broadcast(wide),
                                             idxf[:].unsqueeze(3).to_broadcast(wide), ALU.is_equal)
                elif k == 14:
                    last = dve.tensor_tensor(hot[:], hot[:], w4[:].unsqueeze(3).to_broadcast(wide), ALU.mult)
                elif k == 15:
                    last = dve.tensor_tensor(hot[:, :, 0:2], hot[:, :, 0:2], hot[:, :, 2:4], ALU.add)
                else:
                    last = dve.tensor_tensor(wtok[:], hot[:, :, 0], hot[:, :, 1], ALU.add)
                last.then_inc(s["r_dve"], 1)
                if k == 0:
                    dve.wait_ge(s["r_dve"], 17 * J + 1)
                    dve.sem_inc(s["misc_read"], 1)

            def expert_major(J):
                dve.wait_ge(s["misc_pe"], USE[("wT", J)] + 1)
                if J:
                    dve.wait_ge(s["w_st"], 16 * J)
                dve.tensor_copy(wTs[:], misc[0:NE, :]).then_inc(s["wt_dve"], 1)
                dve.wait_ge(s["wt_dve"], J + 1)
                dve.sem_inc(s["misc_read"], 1)

            def dve_task(task, *a):
                if task == "stats":
                    dve.wait_ge(x_in_s[a[0]], 16)
                    if a[0]:
                        dve.wait_ge(s["ag_done"], TJ * a[0])
                    statistics("st_done", 0, *a)
                elif task == "stats2":
                    dve.wait_ge(s["misc_read"], USE[("y", a[0])] + 1)
                    statistics("st2", 1, *a)
                elif task == "aggr":
                    aggregate("st_done", "ag_done", "xn_done", 0, *a)
                elif task == "aggr2":
                    aggregate("st2", "ag2", "xn2", 1, *a)
                elif task == "norm":
                    normalise("rstd_done", "xn_done", "xT", 0, *a)
                elif task == "norm2":
                    normalise("rstd2", "xn2", "xT2", 1, *a)
                elif task in ("q", "qf", "k", "kf"):
                    rope_product(task, *a)
                else:
                    {"max": split_max, "sums": out_sums, "out": out_scaled, "r1": rest, "p3": third, "y": residual,
                     "low": low, "route": route, "wT": expert_major}[task](*a)

            for v in range(FIRST, LAST + 1):
                small = tasks("dve", v)
                q = v + LEAD
                if 0 <= q < NSTEP:
                    for h in range(HG):
                        dve_max(q, h)
                        if h == HG - 1 and q + 1 in END:
                            last_max(END.index(q + 1))
                        for task in small[h:h + 1]:
                            dve_task(*task)
                    small = small[HG:]
                for task in small:
                    dve_task(*task)

            def low_parts(e, buf, slot):
                dve.wait_ge(s["eh_act"], 2 * e + 1)
                dve.tensor_tensor(elo[:, buf, :, :].rearrange("p a d -> p (a d)"), pair[slot][:, 0, 0:2 * D],
                                  ehi[:, buf, :, :].rearrange("p a d -> p (a d)").bitcast(F32), ALU.subtract)\
                    .then_inc(s["el_dve"], 1)

            def hidden(e, J, slot):
                n = e * NJ + J
                b = J % 2
                dve.wait_ge(s["th_act"], n + 1)
                dve.wait_ge(s["hh_dve"], n + 1)
                dve.scalar_tensor_tensor(ga[:, b, :], th[:, b, :], 1.0, pair[slot][:, 0, :], ALU.add, ALU.mult)\
                    .then_inc(s["ga_dve"], 1)
                dve.wait_ge(s["ga_dve"], n + 3)
                dve.wait_ge(s["hw_pool"], n + 1)
                dve.tensor_tensor(hh[:, b, :], ga[:, b, :], pair[slot][:, 1, :], ALU.mult).then_inc(s["hh_dve"], 1)

            for b in range(2):
                dve.memset(ga[:, b, 0:1], 0.0).then_inc(s["ga_dve"], 1)
                dve.memset(hh[:, b, 0:1], 0.0).then_inc(s["hh_dve"], 1)
            low_parts(0, 0, 1)
            with dve.Fori(0, NX // 2) as i:
                for k in range(2):
                    e = 2 * i
                    hidden(e + k, 0, k)
                    hidden(e + k, 1, 1 - k)
                    hidden(e + k, 2, k)
                    low_parts(e + (k + 1), 1 - k, 1 - k)
                    hidden(e + k, 3, k)
            for J in range(NJ):
                cols = slice(J * TJ, (J + 1) * TJ)
                dve.wait_ge(s["ft_pe"], J + 1)
                dve.tensor_tensor(yo[:, cols, :], xs[:, cols, :],
                                  pair[J // 2][:, J % 2, :].rearrange("p (i d) -> p i d", i=TJ), ALU.add)\
                    .then_inc(s["yo_dve"], 1)


_INS = ["L0_attn_x", "L0_attn_W_Q", "L0_attn_W_K", "L0_attn_W_V", "L0_attn_W_O", "L0_ffn_router_w",
        "L0_ffn_router_bias", "L0_ffn_gate_w", "L0_ffn_up_w", "L0_ffn_down_w", "L0_ffn_sgate_w", "L0_ffn_sup_w",
        "L0_ffn_sdown_w"]


def rope_tables():
    theta = np.float32(1.0) / np.float32(10000.0) ** (np.arange(0, DK, 2, dtype=np.float32) / np.float32(DK))
    ang = np.outer(np.arange(S, dtype=np.float32), theta.astype(np.float32)).astype(np.float32)
    ang = np.concatenate([ang, ang], axis=1).T
    sign = np.where(np.arange(DK) < DK // 2, -1.0, 1.0).astype(np.float32)[:, None]
    cos, sin = np.cos(ang).astype(np.float32), (np.sin(ang).astype(np.float32) * sign).astype(np.float32)
    return np.repeat(cos, NH, axis=0), np.repeat(sin, NH, axis=0)


def kernel(**inputs):
    import concourse.bacc as _bacc
    from concourse.bass_utils import run_bass_kernel_spmd as _run

    nc = _bacc.Bacc("TRN2", target_bir_lowering=False, num_devices=1)
    arrays, args = {}, []
    cos, sin = rope_tables()
    for name, a in [(n, inputs[n]) for n in _INS] + [("rope_cos", cos), ("rope_sin", sin)]:
        a = np.ascontiguousarray(a)
        arrays[f"in_{name}"] = a
        args.append(nc.dram_tensor(f"in_{name}", a.shape, mybir.dt.from_np(a.dtype), kind="ExternalInput").ap())
    args.append(nc.dram_tensor("out_0", (1, S, D), F32, kind="ExternalOutput").ap())
    mixer(nc, *args)
    r = _run(nc, [arrays], core_ids=[0])
    return r.results[0]["out_0"]
```

```python
from contextlib import ExitStack

import numpy as np

import concourse.bass as bass
from concourse import mybir

ALU = mybir.AluOpType
ACT = mybir.ActivationFunctionType
AX = mybir.AxisListType.X
F32 = mybir.dt.float32
F32R = mybir.dt.float32r
BF16 = mybir.dt.bfloat16
U32 = mybir.dt.uint32

P = 128
S = 2048
D = 128
NH = 16
DK = D // NH
HG = 4
NG = NH // HG
NT = S // P
BT = 512
NJ = S // BT
TJ = BT // P
NE = 32
TOPK = 4
NSH = 4
NX = NE + NSH
PIECES = 3
MROW = PIECES * PIECES * DK
SCALE = float(1.0 / np.sqrt(np.float32(DK)))
BIG = 1.0e30
EPS = 1e-5
TWO_ONES = float(np.array([0x3F803F80], np.uint32).view(np.float32)[0])

GROUPS = [(J, G) for J in range(NJ) for G in range(NG)]
STEPS = [(b, J, G, t) for b, (J, G) in enumerate(GROUPS) for t in range(TJ * (J + 1))]
NSTEP = len(STEPS)
END = [sum(TJ * (J + 1) for J, _ in GROUPS[:b + 1]) for b in range(len(GROUPS))]
NB = len(GROUPS)
START = [0] + END[:-1]
LEAD = 7
SCANS = [(b, i, c, h, m) for b, (J, G) in enumerate(GROUPS) for c in range(J + 1) for i in range(TJ)
         for m in (max(TJ // (i + 1), 1) if c == J else 1,) for h in range(0, HG, m)]
SCANNED = [sum(s[0] <= b for s in SCANS) for b in range(NB)]
DVE_ROUTE = 14
LAG = 3
NPROB = 4


def scan_steps():
    by = [(START[0] - LEAD - END[0], 0)] + [(START[b] - LEAD, SCANNED[b]) for b in (*range(0, NB, NG), NB - 1)]
    at, q = {}, 0
    for (v0, q0), (v1, q1) in zip(by, by[1:]):
        for v in range(v0, v1):
            upto = q0 + -(-(q1 - q0) * (v + 1 - v0) // (v1 - v0))
            at[v] = list(range(q, upto))
            q = upto
    return at


SCAN_AT = scan_steps()
SCAN_END = [next(v + 1 for v, scans in SCAN_AT.items() if SCANNED[b] - 1 in scans) for b in range(NB)]


MOE = NSTEP + LAG
HEAD = [(0, 0), (0, 1), (0, 2), (1, 0), (1, 1), (0, 3), (1, 2), (1, 3)] + [(e, J) for e in range(2, NSH) for J in range(NJ)]
TURN_AT = {2: 1, 7: 2, 11: 3, 15: 4}
SLOTS = {}
for use in [("turn", 0)] + [u for m in range(len(HEAD)) for u in ([("turn", TURN_AT[m])] if m in TURN_AT else []) + [("block", m)]]:
    k = len(SLOTS)
    SLOTS[use] = ((k + 1) % 2, list(SLOTS)[k - 2] if k >= 2 else None)


def plan():
    at = {e: {} for e in ("pe", "act", "dve", "pool", "sp")}
    taken = {}

    def pe(v, task):
        while v in taken:
            v += 1
        taken[v] = task
        at["pe"].setdefault(v, []).append(task)
        return v

    def on(engine, v, *task):
        at[engine].setdefault(v, []).append(task)

    for b in range(NB):
        v = pe(SCAN_END[b], ("max", b))
        on("act", v + 1, "max", b)
        on("pool", v + 1, "max", b)
        on("sp", v + 2, "max", b)
    for b in range(NB):
        v = pe(END[b] + LAG, ("out", b))
        on("dve", v + (b < NB - 1), "sums", b)
        on("dve", v + (b < NB - 1), "out", b)

    def prepare_early(J, v):
        on("dve", v - 3, "stats", J)
        on("dve", v - 3, "aggr", J)
        on("pool", v - 2, "rstd", J)
        on("dve", v - 1, "norm", J)
        v = pe(v, ("xT", J))
        on("act", v + 1, "xT", J)
        on("pe", v + 2, "qk", J)
        for task in ("q", "qf", "k", "kf"):
            on("dve", v + 3, task, J)
        on("pool", v + 4, "rope", J, 0)
        on("pool", v + 4, "rope", J, 1)
        for side in range(2):
            on("act", v + 5 + side, "p1", J, side)
            on("dve", v + 6 + side, "r1", J, side)
            on("act", v + 7 + side, "p2", J, side)
            on("dve", v + 8 + side, "p3", J, side)
        on("sp", v + 9, "pieces", J)
        on("sp", v + 9, "stacks", J)
        w = pe(v + 3, ("v", J))
        on("act", w + 4, "v", J)

    def prepare(J, v):
        on("dve", v - 6, "stats", J)
        on("dve", v - 5, "aggr", J)
        on("pool", v - 4, "rstd", J)
        on("pool", v - 3, "norm", J)
        v = pe(v, ("xT", J))
        on("act", v + 1, "xT", J)
        v = pe(v + 2, ("q", J))
        on("dve", v + 1, "q", J)
        v = pe(v + 1, ("qf", J))
        on("dve", v + 1, "qf", J)
        on("pool", v + 1, "rope", J, 0)
        v = pe(v + 1, ("k", J))
        on("dve", v + 1, "k", J)
        on("act", v + 2, "p1", J, 0)
        v = pe(v + 1, ("kf", J))
        on("dve", v + 1, "kf", J)
        on("pool", v + 1, "rope", J, 1)
        on("pool", v + 2, "r1", J, 0)
        on("act", v + 3, "p1", J, 1)
        on("act", v + 3, "p2", J, 0)
        on("pool", v + 4, "r1", J, 1)
        on("pool", v + 4, "p3", J, 0)
        on("act", v + 5, "p2", J, 1)
        on("pool", v + 6, "p3", J, 1)
        on("sp", v + 6, "pieces", J)
        w = pe(v + 1, ("v", J))
        on("act", w + 1, "v", J)
        on("sp", max(v + 6, END[4 * J - 5] + LAG + 1), "stacks", J)

    def finish(J, v):
        v = pe(v, ("aT", J))
        on("act", v + 1, "aT", J)
        v = pe(v + 2, ("y", J))
        on("dve", v + 1, "y", J)
        on("dve", v + 2, "stats2", J)
        on("dve", v + 3, "aggr2", J)
        on("pool", v + 4, "rstd2", J)
        on("pool", v + 5, "norm2", J)
        v = pe(v + 6, ("xT2", J))
        on("act", v + 1, "xT2", J)
        on("pool", v + 2, "low", J)
        v = pe(v + 2, ("lg", J))
        for k in range(3):
            on("dve", v + 1 + k, "route", J, k)
        on("act", v + 4, "route", J)
        for k in range(3, DVE_ROUTE):
            on("dve", v + 5 + (k - 3) // 2, "route", J, k)
        on("pool", v + 11, "route", J)
        v = pe(v + 13, ("wT", J))
        on("act", v + 1, "wT", J)
        on("sp", v + 1, "wT", J)

    prepare_early(0, -40)
    prepare_early(1, -32)
    for J in range(1, NJ):
        on("pool", -20, "behind", J)
    prepare(2, 8)
    prepare(3, 44)
    for J in range(NJ - 1):
        finish(J, END[4 * J + 3] + LAG + 2)
    J = NJ - 1
    pe(MOE + 1, ("aT", J))
    on("act", MOE + 1, "aT", J)
    pe(MOE + 2, ("y", J))
    for task in ("y", "stats2", "aggr2"):
        on("dve", MOE + 2, task, J)
    on("pool", MOE + 2, "rstd2", J)
    on("dve", MOE + 3, "norm2", J)
    pe(MOE + 4, ("xT2", J))
    on("act", MOE + 4, "xT2", J)
    on("dve", MOE + 4, "low", J)
    pe(MOE + 5, ("lg", J))
    on("act", MOE + 5, "route", J)
    for k in range(DVE_ROUTE):
        on("dve", MOE + 5 + (k + 1) // 4, "route", J, k)
    on("pool", MOE + 9, "route", J)
    on("pe", MOE + 11, "wT", J)
    on("act", MOE + 11, "wT", J)
    on("sp", MOE - 5, "expert", 0)
    on("sp", MOE - 5, "expert", 1)
    on("sp", MOE + 1, "expert", 2)
    on("sp", MOE + 3, "expert", 3)
    on("sp", MOE + 11, "wT", J)
    first = min(min(a) for a in at.values())
    last = max(max(a) for a in at.values())
    order = {task: n for n, (v, task) in enumerate(sorted(taken.items()))}
    return at, order, first, last


AT, USE, FIRST, LAST = plan()


def mixer(nc, x_in, wq_in, wk_in, wv_in, wo_in, rw_in, rb_in, gw_in, uw_in, dw_in, sg_in, su_in, sd_in,
          cos_in, sin_in, out):
    with ExitStack() as ctx:
        def sb(name, shape, dt, to=ctx):
            return to.enter_context(nc.sbuf_tensor(name, shape, dt))

        def sem(name):
            return ctx.enter_context(nc.semaphore(name))

        qp_d = nc.dram_tensor("qp_d", [NJ, PIECES, P, BT], BF16).ap()
        kp_d = nc.dram_tensor("kp_d", [NJ, 2 * PIECES - 1, P, BT], BF16).ap()
        zero_d = nc.dram_tensor("zero_d", [PIECES, NH * BT], BF16).ap()
        wt_d = nc.dram_tensor("wt_d", [NX, S], F32).ap()

        xs = sb("xs", [P, NT, D], F32)
        ident = sb("ident", [P, P], F32)
        negI = sb("negI", [P, P], BF16)
        later_k = sb("later_k", [P, P], BF16)
        iota_e = sb("iota_e", [P, NE], F32)
        iota_i = sb("iota_i", [P, NE], mybir.dt.int32)
        xh = sb("xh", [P, S], F32R)
        xl = sb("xl", [P, S], F32R)
        zb = sb("zb", [P, P], BF16)
        zr = sb("zr", [P, BT], BF16)
        rwT = sb("rwT", [P, NE], F32)
        bias = sb("bias", [P, NE], F32)
        wT = sb("wT", [P, 6, D], F32)

        attn_mem = ExitStack()
        kst = sb("kst", [P, NJ, NH, BT], BF16, attn_mem)
        qst = sb("qst", [P, 2, NH, BT], BF16, attn_mem)
        vext = sb("vext", [P, NT, NH, DK + 1], F32, attn_mem)
        prob = sb("prob", [P, NPROB, HG, BT], F32, attn_mem)
        cos_t = [sb("cos_t", [P, BT], F32, attn_mem)[:], prob[:, 1, 0, :]]
        sin_t = [sb("sin_t", [P, BT], F32, attn_mem)[:], prob[:, 1, 1, :]]
        ccos = sb("ccos", [P, 2, BT], F32, attn_mem)
        csin = sb("csin", [P, 2, BT], F32, attn_mem)
        piece = sb("piece", [P, 2, PIECES, BT], BF16, attn_mem)
        xn = sb("xn", [P, 2, TJ, D], F32, attn_mem)
        xnT = sb("xnT", [P, BT], F32, attn_mem)
        xfT = sb("xfT", [P, BT], F32, attn_mem)
        attn = sb("attn", [P, TJ, D], F32, attn_mem)
        ot = sb("ot", [P, BT], F32, attn_mem)
        pmax = sb("pmax", [P, 2, HG, TJ, NJ], F32, attn_mem)
        negm = sb("negm", [P, 2, HG * TJ], F32, attn_mem)
        mrow = sb("mrow", [HG * TJ, 2, P], F32, attn_mem)
        mp = sb("mp", [HG * TJ, PIECES, P], BF16, attn_mem)
        rsum = sb("rsum", [P, TJ, HG], F32, attn_mem)
        half = sb("half", [NSH, BT], F32, attn_mem)
        stats = sb("stats", [P, 2, TJ, 6], F32, attn_mem)
        mv = sb("mv", [P, 2, TJ, 2], F32, attn_mem)
        veps = sb("veps", [P, 2, TJ], F32, attn_mem)
        rstd = sb("rstd", [P, 2, TJ], F32, attn_mem)
        mhalf = sb("mhalf", [P, TJ], F32, attn_mem)
        wnat = prob[:, 0, 0, :].rearrange("p (k d) -> p k d", k=4)
        rwn = prob[0:NE, 0, 1, 0:D]
        lg = sb("lg", [P, TJ, NE], F32, attn_mem)
        ex = sb("ex", [P, TJ, NE], F32, attn_mem)
        sc = sb("sc", [P, TJ, NE], F32, attn_mem)
        mx = sb("mx", [P, TJ], F32, attn_mem)
        sm = sb("sm", [P, TJ], F32, attn_mem)
        rs = sb("rs", [P, TJ], F32, attn_mem)
        top = sb("top", [P, TJ, 8], F32, attn_mem)
        idx = sb("idx", [P, TJ, 8], U32, attn_mem)
        idxf = sb("idxf", [P, TJ, TOPK], F32, attn_mem)
        ts4 = sb("ts4", [P, TJ], F32, attn_mem)
        tc4 = sb("tc4", [P, TJ], F32, attn_mem)
        tr4 = sb("tr4", [P, TJ], F32, attn_mem)
        w4 = sb("w4", [P, TJ, TOPK], F32, attn_mem)
        hot = sb("hot", [P, TJ, TOPK, NE], F32, attn_mem)
        wtok = sb("wtok", [P, TJ, NE], F32, attn_mem)
        wTs = sb("wTs", [P, P], F32, attn_mem)
        attn_mem.close()

        ewn = sb("ewn", [P, 2, 3, D], F32)
        ehi = sb("ehi", [P, 2, 2, D], F32R)
        elo = sb("elo", [P, 2, 2, D], F32R)
        edn = sb("edn", [P, 2, D], F32)
        wrow = sb("wrow", [1, 2, S], F32)
        th = sb("th", [P, 2, BT], F32)
        ga = sb("ga", [P, 2, BT], F32)
        hh = sb("hh", [P, 2, BT], F32)
        hw = sb("hw", [P, NJ, BT], F32)
        wb = sb("wb", [P, 2, S], F32)
        fin = sb("fin", [P, NJ, BT], F32)
        yo = sb("yo", [P, NT, D], F32)

        bank = [ctx.enter_context(nc.psum_tensor(f"bank{i}", [P, 512], F32)) for i in range(2)]
        pair = [ctx.enter_context(nc.psum_tensor(f"pair{i}", [P, 2, 512], F32)) for i in range(2)]
        accb = ctx.enter_context(nc.psum_tensor("accb", [P, 512], F32))
        misc = ctx.enter_context(nc.psum_tensor("misc", [P, 512], F32))

        names = """w_in rw_in c_mem c_done stk_dve stk_pool vc_z z_store half_m half_st misc_pe misc_read
            proj_pe proj_read wt_pe wt_act rwt_pe rwt_dve st_done ag_done ve_done rstd_done xn_done
            rp_sin rp_add rp_p1 rp_r1 rp_p2 rp_p3 mm_pe mx_rd mx_fin ms_part ms_done m_row qk_pe
            ex_act caus_pool av_pe ot_act rs_out at_done st2 ag2 ve2 rstd2 xn2 xh_act low_done r_dve
            r_pool r_act wt_done wt3_pe w_st et_pe eh_act el_dve gt_pe gu_pe th_act ga_dve hh_dve
            hw_pool wb_pool dn_pe z_pool fin_act ft_pe yo_dve o_st acc0""".split()
        s = {n: sem(n) for n in names}
        x_in_s = [sem(f"x_in{J}") for J in range(NJ)]
        tab_in = [sem(f"tab_in{J}") for J in range(NJ)]
        p_store = [sem(f"p_store{J}") for J in range(NJ)]
        stk_first = sem("stk_first")
        stk_in = [sem(f"stk_in{J}") for J in range(NJ)]
        ew_in = [sem(f"ew_in{k}") for k in range(2)]
        wr_in = [sem(f"wr_in{k}") for k in range(2)]

        out_bank = [bank[0], bank[1], accb, misc]

        block = ctx.enter_context(nc.Block())
        LOADS = 2 * PIECES + 1

        def tok(J):
            return slice(J * BT, (J + 1) * BT)

        def tasks(engine, v):
            return AT[engine].get(v, [])

        @block.sync
        def _(sp):
            for J in range(NJ):
                sp.dma_start(xs[:, J * TJ:(J + 1) * TJ, :],
                             x_in[0, tok(J), :].rearrange("(t p) d -> p t d", p=P)).then_inc(x_in_s[J], 16)
                if J < 2:
                    sp.dma_start(cos_t[J % 2], cos_in[:, tok(J)]).then_inc(tab_in[J], 16)
                    sp.dma_start(sin_t[J % 2], sin_in[:, tok(J)]).then_inc(tab_in[J], 16)
            sp.wait_ge(s["stk_pool"], 1)
            sp.dma_start(zero_d, qst[96:96 + PIECES, 0].rearrange("p h s -> p (h s)")).then_inc(s["z_store"], 16)
            sp.wait_ge(s["half_m"], 1)
            for J in range(NJ):
                sp.dma_start(wt_d[0:NSH, tok(J)], half[:]).then_inc(s["half_st"], 16)

            def pieces(J):
                for side, dst in ((0, qp_d), (1, kp_d)):
                    sp.wait_ge(s["rp_p3"], 2 * J + side + 1)
                    sp.dma_start(dst[J, 0:PIECES].rearrange("c p s -> p c s"), piece[:, side, :, :])\
                        .then_inc(p_store[J], 16)
                sp.dma_start(kp_d[J, PIECES:].rearrange("c p s -> p c s"), piece[:, 1, 0:PIECES - 1, :])\
                    .then_inc(p_store[J], 16)

            def stacks(J):
                sp.wait_ge(p_store[J], 16 * 3)
                sp.wait_ge(s["z_store"], 16)
                sp.wait_ge(s["stk_dve"], min(J, 1) + 1)
                sp.wait_ge(s["stk_pool"], J + 1)
                if J >= 2:
                    sp.wait_ge(s["av_pe"], END[4 * J - 5])
                for h0, h1, done in ((0, HG, stk_first), (HG, NH, stk_in[0])) if J == 0 else ((0, NH, stk_in[J]),):
                    for r in range(PIECES):
                        rows = slice(r * PIECES * DK, (r + 1) * PIECES * DK)
                        sp.dma_start(kst[rows, J, h0:h1],
                                     kp_d[J, r:r + PIECES].rearrange("c (r h) s -> (c r) h s", h=NH)[:, h0:h1])\
                            .then_inc(done, 16)
                        sp.dma_start(qst[rows, J % 2, h0:h1],
                                     qp_d[J].rearrange("c (r h) s -> (c r) h s", h=NH)[:, h0:h1]).then_inc(done, 16)
                    sp.dma_start(qst[MROW:MROW + PIECES, J % 2, h0:h1],
                                 zero_d.rearrange("c (h s) -> c h s", h=NH)[:, h0:h1]).then_inc(done, 16)
                if J in (0, 2):
                    K = {0: 2, 2: 3}[J]
                    sp.dma_start(cos_t[0], cos_in[:, tok(K)]).then_inc(tab_in[K], 16)
                    sp.dma_start(sin_t[0], sin_in[:, tok(K)]).then_inc(tab_in[K], 16)

            def store_m(b):
                J, G = GROUPS[b]
                sp.wait_ge(s["ms_done"], b + 1)
                for c in range(PIECES):
                    sp.dma_start(qst[MROW + c:MROW + c + 1, J % 2, G * HG:(G + 1) * HG].rearrange("c h s -> c (h s)"),
                                 mp[:, c, :]).then_inc(s["m_row"], 16)

            def store_w(J):
                sp.wait_ge(s["wt_done"], J + 1)
                for i in range(TJ):
                    sp.dma_start(wt_d[NSH:, (J * TJ + i) * P:(J * TJ + i + 1) * P], wTs[i * NE:(i + 1) * NE, :])\
                        .then_inc(s["w_st"], 16)

            def expert_weights(buf, g, u, d):
                for k, w in enumerate((g, u, d)):
                    sp.dma_start(ewn[:, buf, k, :], w).then_inc(ew_in[buf], 16)

            def row(buf, w):
                sp.dma_start(wrow[:, buf, :], w).then_inc(wr_in[buf], 16)

            def shared(c):
                if c == 0:
                    sp.wait_ge(s["qk_pe"], 2 * (NSTEP - TJ))
                    sp.wait_ge(s["half_st"], 16 * NJ)
                if c >= 2:
                    sp.wait_ge(s["et_pe"], c - 1)
                    sp.wait_ge(s["wb_pool"], c - 1)
                h = slice(c * D, (c + 1) * D)
                expert_weights(c % 2, sg_in[h, :], su_in[h, :], sd_in[:, h])
                row(c % 2, wt_d[c:c + 1, :])

            for v in range(FIRST, LAST + 1):
                for task, *a in tasks("sp", v):
                    {"pieces": pieces, "stacks": stacks, "max": store_m, "wT": store_w, "expert": shared}[task](*a)

            sp.wait_ge(s["w_st"], 16 * TJ * NJ)
            with sp.Fori(0, NE // 2) as i:
                for k in range(2):
                    e = 2 * i
                    sp.wait_ge(s["et_pe"], e + (NSH + k - 1))
                    sp.wait_ge(s["wb_pool"], e + (NSH + k - 1))
                    one = bass.ds(e + k, 1)
                    expert_weights(k, *(w[one, :, :].rearrange("a p d -> (a p) d") for w in (gw_in, uw_in, dw_in)))
                    row(k, wt_d[bass.ds(e + (NSH + k), 1), :])
            sp.wait_ge(s["et_pe"], NX - 1)
            sp.wait_ge(s["wb_pool"], NX - 1)
            expert_weights(0, gw_in[0], uw_in[0], dw_in[0])
            row(0, wt_d[0:1, :])
            for J in range(NJ):
                sp.wait_ge(s["yo_dve"], J + 1)
                sp.dma_start(out[0, tok(J), :].rearrange("(t p) d -> p t d", p=P),
                             yo[:, J * TJ:(J + 1) * TJ, :]).then_inc(s["o_st"], 16)
            sp.wait_ge(s["o_st"], 16 * NJ)

        @block.gpsimd
        def _(pool):
            pool.memset(ident[:], 0.0).then_inc(s["c_mem"], 1)
            pool.memset(negI[:], 0.0).then_inc(s["c_mem"], 1)
            pool.memset(later_k[:], 1.0).then_inc(s["c_mem"], 1)
            pool.wait_ge(s["c_mem"], 3)
            pool.affine_select(out=ident[:], in_=ident[:], compare_op=ALU.not_equal, fill=1.0, base=0,
                               pattern=[[-1, P]], channel_multiplier=1).then_inc(s["c_done"], 1)
            pool.affine_select(out=negI[:], in_=negI[:], compare_op=ALU.not_equal, fill=-BIG, base=0,
                               pattern=[[-1, P]], channel_multiplier=1).then_inc(s["c_done"], 1)
            pool.affine_select(out=later_k[:], in_=later_k[:], compare_op=ALU.is_gt, fill=0.0, base=0,
                               pattern=[[1, P]], channel_multiplier=-1).then_inc(s["c_done"], 1)
            pool.iota(iota_i[:], pattern=[[1, NE]], base=0, channel_multiplier=0).then_inc(s["c_done"], 1)
            pool.memset(half[:], 0.5).then_inc(s["half_m"], 1)
            pool.memset(mhalf[:], -0.5).then_inc(s["half_m"], 1)
            pool.wait_ge(s["c_done"], 4)
            pool.wait_ge(s["half_m"], 2)

            def rstd_of(ag, ve, done, which, J):
                pool.wait_ge(s[ag], TJ * (J + 1))
                pool.tensor_scalar(veps[:, which, :], mv[:, which, :, 1], EPS, 0.0, ALU.add, ALU.add).then_inc(s[ve], 1)
                pool.wait_ge(s[ve], J + 1)
                pool.tensor_tensor(rstd[:, which, :], veps[:, which, :], mhalf[:], ALU.pow).then_inc(s[done], 1)

            def rope(J, side):
                pool.wait_ge(s["rp_sin"], 2 * J + side + 1)
                pool.tensor_tensor(ccos[:, side, :], ccos[:, side, :], csin[:, side, :], ALU.add).then_inc(s["rp_add"], 1)

            def normalise(rst, done, task, which, J):
                pool.wait_ge(s[rst], J + 1)
                if J:
                    pool.wait_ge(s["misc_pe"], USE[(task, J - 1)] + 1)
                for i in range(TJ):
                    last = pool.tensor_scalar(xn[:, which, i, :], xs[:, J * TJ + i, :], mv[:, which, i, 0:1],
                                              rstd[:, which, i:i + 1], ALU.subtract, ALU.mult)
                last.then_inc(s[done], 1)

            def causal(u):
                b, J, G, t = STEPS[u]
                if t >= TJ * J:
                    own = prob[:, u % NPROB, :, (t - TJ * J) * P:(t - TJ * J + 1) * P]
                    pool.wait_ge(s["ex_act"], 2 * u + 2)
                    pool.affine_select(out=own, in_=own, compare_op=ALU.is_ge, fill=0.0, base=0,
                                       pattern=[[0, HG], [1, P]], channel_multiplier=-1).then_inc(s["caus_pool"], 1)

            def rest(J, side):
                pool.wait_ge(s["rp_p1"], 2 * J + side + 1)
                pool.tensor_tensor(csin[:, side, :], ccos[:, side, :], piece[:, side, 0, :], ALU.subtract)\
                    .then_inc(s["rp_r1"], 1)

            def third(J, side):
                pool.wait_ge(s["rp_p2"], 2 * J + side + 1)
                pool.tensor_tensor(piece[:, side, 2, :], csin[:, side, :], piece[:, side, 1, :], ALU.subtract)\
                    .then_inc(s["rp_p3"], 1)

            def low(J):
                pool.wait_ge(s["xh_act"], J + 1)
                pool.tensor_tensor(xl[:, tok(J)], xfT[:], xh[:, tok(J)].bitcast(F32), ALU.subtract).then_inc(s["low_done"], 1)

            def split_max(b):
                pool.wait_ge(s["misc_read"], USE[("max", b)] + 1)
                if b:
                    pool.wait_ge(s["m_row"], 16 * PIECES * b)
                pool.tensor_copy(mp[:, 0, :], mrow[:, 0, :]).then_inc(s["ms_part"], 1)
                pool.wait_ge(s["ms_part"], 3 * b + 1)
                pool.tensor_tensor(mrow[:, 1, :], mrow[:, 0, :], mp[:, 0, :], ALU.subtract).then_inc(s["ms_part"], 1)
                pool.wait_ge(s["ms_part"], 3 * b + 2)
                pool.tensor_copy(mp[:, 1, :], mrow[:, 1, :]).then_inc(s["ms_part"], 1)
                pool.wait_ge(s["ms_part"], 3 * b + 3)
                pool.tensor_tensor(mp[:, 2, :], mrow[:, 1, :], mp[:, 1, :], ALU.subtract).then_inc(s["ms_done"], 1)

            def weigh_experts(J):
                pool.wait_ge(s["r_dve"], DVE_ROUTE * (J + 1))
                pool.tensor_tensor(hot[:], hot[:], w4[:].unsqueeze(3).to_broadcast([P, TJ, TOPK, NE]), ALU.mult)\
                    .then_inc(s["r_pool"], 1)
                pool.wait_ge(s["r_pool"], 3 * J + 1)
                pool.tensor_tensor(hot[:, :, 0:2], hot[:, :, 0:2], hot[:, :, 2:4], ALU.add).then_inc(s["r_pool"], 1)
                pool.wait_ge(s["r_pool"], 3 * J + 2)
                if J:
                    pool.wait_ge(s["misc_pe"], USE[("wT", J - 1)] + 1)
                pool.tensor_tensor(wtok[:], hot[:, :, 0], hot[:, :, 1], ALU.add).then_inc(s["r_pool"], 1)

            def pool_tasks(v):
                for task, *a in tasks("pool", v):
                    if task in ("norm", "norm2"):
                        two = task == "norm2"
                        normalise(("rstd_done", "rstd2")[two], ("xn_done", "xn2")[two], ("xT", "xT2")[two], two * 1, *a)
                    elif task in ("r1", "p3", "low", "max", "route", "behind"):
                        {"behind": behind, "r1": rest, "p3": third, "low": low, "max": split_max, "route": weigh_experts}[task](*a)
                    elif task == "rstd":
                        rstd_of("ag_done", "ve_done", "rstd_done", 0, *a)
                    elif task == "rstd2":
                        rstd_of("ag2", "ve2", "rstd2", 1, *a)
                    else:
                        rope(*a)

            pool.memset(vext[:, :, :, DK:DK + 1], 1.0).then_inc(s["vc_z"], 1)
            pool.memset(zb[:], 0.0).then_inc(s["z_pool"], 1)
            pool.memset(zr[:], 0.0).then_inc(s["z_pool"], 1)
            pool.wait_ge(s["z_pool"], 2)
            pool.wait_ge(s["vc_z"], 1)
            pool.memset(qst[64:P, 0].rearrange("p h s -> p (h s)").bitcast(F32), 0.0).then_inc(s["stk_pool"], 1)
            pool.wait_ge(s["stk_pool"], 1)

            def behind(J):
                pool.wait_ge(s["rp_add"], 4)
                rows, value = (qst[64:P, 1], 0.0) if J == 1 else (kst[64:P, J], TWO_ONES)
                pool.memset(rows.rearrange("p h s -> p (h s)").bitcast(F32), value).then_inc(s["stk_pool"], 1)
                pool.wait_ge(s["stk_pool"], J + 1)

            def row_ready(i, buf, done):
                pool.wait_ge(wr_in[buf], 16 * i + 16)
                pool.wait_ge(s["hw_pool"], done)

            def spread(buf):
                pool.partition_broadcast(wb[:, buf, :], wrow[:, buf, :]).then_inc(s["wb_pool"], 1)

            def weigh(e, buf, J, m, k):
                pool.wait_ge(s["hh_dve"], m + 1)
                if J == 0:
                    pool.wait_ge(s["wb_pool"], e + 1)
                if not isinstance(m, int) or m >= NJ:
                    pool.wait_ge(s["dn_pe"], m - (NJ - 1))
                pool.tensor_tensor(hw[:, k, :], hh[:, k % 2, :], wb[:, buf, tok(J)], ALU.mult)\
                    .then_inc(s["hw_pool"], 1)

            for v in range(FIRST, MOE + len(HEAD)):
                pool_tasks(v)
                if 0 <= v < NSTEP:
                    causal(v)
                m = v - MOE
                if m == -1:
                    pool.wait_ge(s["et_pe"], 1)
                    for e in range(2):
                        pool.wait_ge(wr_in[e], 16)
                        spread(e)
                if m < 0:
                    continue
                e, J = HEAD[m]
                weigh(e, e % 2, J, m, m % NJ)
                if (e, J) == (1, 2):
                    row_ready(1, 0, HEAD.index((0, NJ - 1)) + 1)
                    spread(0)
                if e >= 2 and J == 1:
                    row_ready((e + 1) // 2, (e + 1) % 2, e * NJ)
                    spread((e + 1) % 2)
            with pool.Fori(NSH // 2, NX // 2) as i:
                for k in range(2):
                    e = 2 * i + k
                    n = e * NJ
                    weigh(e, k, 0, n, 0)
                    row_ready(i + k, 1 - k, n)
                    weigh(e, k, 1, n + 1, 1)
                    spread(1 - k)
                    weigh(e, k, 2, n + 2, 2)
                    weigh(e, k, 3, n + 3, 3)

        @block.scalar
        def _(act):
            for k, w in enumerate((wq_in, wk_in, wv_in, wo_in)):
                act.dma_start(wnat[:, k, :], w).then_inc(s["w_in"], 16)
            act.dma_start(rwn, rw_in).then_inc(s["rw_in"], 16)
            act.dma_start(bias[:], rb_in.rearrange("(a e) -> a e", a=1).to_broadcast([P, NE])).then_inc(s["rw_in"], 16)

            act.wait_ge(s["wt_pe"], 4)
            for k in range(2):
                src = bank[1][:, k * D:(k + 1) * D]
                act.activation(wT[:, 2 * k, :].rearrange("p (r h) -> p h r", h=NH),
                               src.rearrange("p (h r) -> p h r", h=NH), ACT.Copy).then_inc(s["wt_act"], 1)
                for a in range(2):
                    act.activation(wT[:, 2 * k + 1, a * (D // 2):(a + 1) * (D // 2)].rearrange("p (r h) -> p h r", h=NH),
                                   src.rearrange("p (h a r) -> p h a r", h=NH, a=2)[:, :, 1 - a, :], ACT.Copy)\
                        .then_inc(s["wt_act"], 1)
            act.activation(wT[:, 4:6, :].rearrange("p a d -> p (a d)"), bank[1][:, 2 * D:4 * D], ACT.Copy)\
                .then_inc(s["wt_act"], 1)

            def act_exp(u, p):
                b, J, G, t = STEPS[u]
                c0 = max(t - TJ * J, 0) * P
                act.wait_ge(s["qk_pe"], 2 * u + p + 1)
                if u >= NPROB:
                    act.wait_ge(s["av_pe"], u - NPROB + 1)
                act.activation(prob[:, u % NPROB, 2 * p:2 * p + 2, c0:], pair[p][:, :, c0:], ACT.Exp, scale=SCALE)\
                    .then_inc(s["ex_act"], 1)

            def act_sums(b):
                act.wait_ge(s["av_pe"], END[b])
                if b:
                    act.wait_ge(s["misc_pe"], USE[("out", b - 1)] + 1)
                J, G = GROUPS[b]
                if J and G == 0:
                    act.wait_ge(s["misc_pe"], USE[("y", J - 1)] + 1)
                act.activation(ot[:], accb[:], ACT.Copy).then_inc(s["ot_act"], 1)

            def act_task(task, J, *a):
                if task in ("xT", "v", "aT", "xT2", "max") or task == "wT" and J < NJ - 1:
                    act.wait_ge(s["misc_pe"], USE[(task, J)] + 1)
                if task == "max":
                    if J:
                        act.wait_ge(s["ms_done"], J)
                    act.activation(mrow[:, 0, :], misc[0:HG * TJ, 0:P], ACT.Copy).then_inc(s["misc_read"], 1)
                elif task == "wT":
                    if J:
                        act.wait_ge(s["w_st"], 16 * TJ * J)
                    if J == NJ - 1:
                        act.wait_ge(s["wt3_pe"], 1)
                        act.activation(wTs[:], pair[SLOTS["turn", 3][0]][:, 1, P:2 * P], ACT.Copy).then_inc(s["wt_done"], 1)
                    else:
                        act.activation(wTs[:], misc[:, 0:P], ACT.Copy).then_inc(s["wt_done"], 1)
                        act.wait_ge(s["wt_done"], J + 1)
                        act.sem_inc(s["misc_read"], 1)
                elif task == "xT":
                    act.activation(xnT[:], misc[:], ACT.Copy).then_inc(s["misc_read"], 1)
                elif task == "v":
                    if J == 0:
                        act.wait_ge(s["vc_z"], 1)
                    act.activation(vext[:, J * TJ:(J + 1) * TJ, :, 0:DK],
                                   misc[:].rearrange("p (t h r) -> p t h r", t=TJ, h=NH), ACT.Copy)\
                        .then_inc(s["misc_read"], 1)
                elif task == "aT":
                    act.activation(ot[:], misc[:], ACT.Copy).then_inc(s["misc_read"], 1)
                elif task == "xT2":
                    act.activation(xfT[:], misc[:], ACT.Copy).then_inc(s["misc_read"], 1)
                    act.wait_ge(s["misc_read"], USE[(task, J)] + 1)
                    act.activation(xh[:, tok(J)], xfT[:], ACT.Copy).then_inc(s["xh_act"], 1)
                elif task == "p1":
                    side, = a
                    act.wait_ge(s["rp_add"], 2 * J + side + 1)
                    if J:
                        act.wait_ge(p_store[J - 1], 16 * 3)
                    act.activation(piece[:, side, 0, :], ccos[:, side, :], ACT.Copy).then_inc(s["rp_p1"], 1)
                elif task == "p2":
                    side, = a
                    act.wait_ge(s["rp_r1"], 2 * J + side + 1)
                    act.activation(piece[:, side, 1, :], csin[:, side, :], ACT.Copy).then_inc(s["rp_p2"], 1)
                elif task == "route":
                    act.wait_ge(s["r_dve"], DVE_ROUTE * J + 3)
                    act.activation(ex[:], sc[:], ACT.Exp).then_inc(s["r_act"], 1)

            def turned_weights(e, buf, slot):
                act.wait_ge(s["et_pe"], e + 1)
                act.activation(ehi[:, buf, :, :].rearrange("p a d -> p (a d)"), pair[slot][:, 0, 0:2 * D], ACT.Copy)\
                    .then_inc(s["eh_act"], 1)
                act.activation(edn[:, buf, :], pair[slot][:, 1, 0:D], ACT.Copy).then_inc(s["eh_act"], 1)

            def gate(m, par, slot):
                act.wait_ge(s["gt_pe"], m + 1)
                if not isinstance(m, int) or m >= 2:
                    act.wait_ge(s["ga_dve"], m - 1)
                act.activation(th[:, par, :], pair[slot][:, 0, :], ACT.Tanh, scale=0.5).then_inc(s["th_act"], 1)

            for v in range(FIRST, MOE + len(HEAD)):
                if 0 <= v < NSTEP:
                    act_exp(v, 0)
                for b in range(NB):
                    if v == END[b] - 1 + LAG:
                        act_sums(b)
                m = v - MOE
                if m == -1:
                    turned_weights(0, 0, SLOTS["turn", 0][0])
                if m in TURN_AT:
                    e = TURN_AT[m]
                    turned_weights(e, e % 2, SLOTS["turn", e][0])
                for task, *a in tasks("act", v):
                    act_task(task, *a)
                if m >= 0:
                    gate(m, m % 2, SLOTS["block", m][0])
                if 0 <= v < NSTEP:
                    act_exp(v, 1)
            with act.Fori(NSH // 2, NX // 2) as i:
                for k in range(2):
                    e = 2 * i
                    n = (e + k) * NJ
                    gate(n, 0, k)
                    gate(n + 1, 1, 1 - k)
                    gate(n + 2, 0, k)
                    turned_weights(e + (k + 1), 1 - k, 1 - k)
                    gate(n + 3, 1, k)
            for J in range(NJ):
                act.wait_ge(s["acc0"], J + 1)
                act.activation(fin[:, J, :], out_bank[J][:], ACT.Copy).then_inc(s["fin_act"], 1)

        @block.tensor
        def _(pe):
            def mm(out, a, b, start=True, stop=True, loose=False):
                return nc.tensor.matmul(out, a, b, start=start, stop=stop, skip_group_check=loose)

            pe.wait_ge(s["c_done"], 4)
            pe.wait_ge(s["w_in"], 16 * 4)
            for k in range(4):
                nc.tensor.transpose(bank[1][:, k * D:(k + 1) * D], wnat[:, k, :], ident[:]).then_inc(s["wt_pe"], 1)
            pe.wait_ge(s["rw_in"], 32)
            nc.tensor.transpose(bank[0][:, 0:NE], rwn, ident[0:NE, 0:NE]).then_inc(s["rwt_pe"], 1)
            pe.wait_ge(s["wt_act"], 7)
            pe.wait_ge(s["rwt_dve"], 1)

            def pe_max(q):
                b, i, c, h0, m = SCANS[q]
                J, G = GROUPS[b]
                n = (i + 1) * P if c == J else BT
                if q == 0:
                    pe.wait_ge(stk_first, 16 * LOADS)
                elif SCANS[q - 1][0] != b and G == (J == 0):
                    pe.wait_ge(stk_in[J], 16 * LOADS)
                if q >= 2:
                    pe.wait_ge(s["mx_rd"], q - 1)
                for h in range(m):
                    head = G * HG + h0 + h
                    last = mm(bank[q % 2][:, h * n:(h + 1) * n], qst[:, J % 2, head, i * P:(i + 1) * P],
                              kst[:, c, head, 0:n], stop=c != J)
                    if c == J:
                        last = mm(bank[q % 2][:, h * n + i * P:(h + 1) * n], negI[:], later_k[:], start=False)
                last.then_inc(s["mm_pe"], 1)

            def pe_scores(u, p):
                b, J, G, t = STEPS[u]
                c0 = max(t - TJ * J, 0) * P
                if t == 0:
                    pe.wait_ge(s["m_row"], 16 * PIECES * (b + 1))
                k = 2 * u + p
                if k == 0:
                    pe.wait_ge(s["proj_read"], 4 * 2)
                if k >= 2:
                    pe.wait_ge(s["ex_act"], k - 1)
                for h in range(2):
                    head = G * HG + 2 * p + h
                    last = mm(pair[p][:, h, c0:], kst[:, t // TJ, head, t % TJ * P:(t % TJ + 1) * P],
                              qst[:, J % 2, head, c0:])
                last.then_inc(s["qk_pe"], 1)

            def pe_av(u, half):
                b, J, G, t = STEPS[u]
                if t == 0 and half:
                    return
                c0 = max(t - TJ * J, 0) * P
                mid = BT // 2 if c0 < BT // 2 else (c0 + BT) // 2
                q = slice(0, BT) if t == 0 else slice(c0, mid) if half == 0 else slice(mid, BT)
                if t < TJ * J:
                    pe.wait_ge(s["ex_act"], 2 * u + 2)
                else:
                    pe.wait_ge(s["caus_pool"], TJ * b + (t - TJ * J) + 1)
                if t == 0 and b:
                    pe.wait_ge(s["ot_act"], b)
                for h in range(HG):
                    last = mm(accb[32 * h:32 * h + DK + 1, q], vext[:, t, G * HG + h, :], prob[:, u % NPROB, h, q],
                              start=t == 0, stop=t == TJ * (J + 1) - 1, loose=True)
                if half or t == 0:
                    last.then_inc(s["av_pe"], 1)

            def pe_task(task, n):
                if task == "qk":
                    pe.wait_ge(s["misc_read"], USE[("xT", n)] + 1)
                    for k in range(4):
                        if n:
                            pe.wait_ge(s["proj_read"], 4 * (n - 1) + k + 1)
                        mm(pair[k // 2][:, k % 2, :], wT[:, k, :], xnT[:]).then_inc(s["proj_pe"], 1)
                    return
                if (task, n) == ("wT", NJ - 1):
                    pe.wait_ge(s["r_pool"], 3 * (n + 1))
                    pe.wait_ge(s["eh_act"], 2 * 3 + 2)
                    nc.tensor.transpose(pair[SLOTS["turn", 3][0]][:, 1, P:2 * P], wtok[:].rearrange("p t e -> p (t e)"),
                                        ident[:]).then_inc(s["wt3_pe"], 1)
                    return
                use = USE[(task, n)]
                if use:
                    pe.wait_ge(s["misc_read"], use)
                if task == "max":
                    pe.wait_ge(s["mx_fin"], n + 1)
                    last = nc.tensor.transpose(misc[0:HG * TJ, 0:P], negm[:, n % 2, :], ident[:])
                elif task == "out":
                    pe.wait_ge(s["ot_act"], n + 1)
                    for i in range(TJ):
                        last = nc.tensor.transpose(misc[:, i * P:(i + 1) * P], ot[:, i * P:(i + 1) * P], ident[:])
                elif task in ("xT", "xT2"):
                    pe.wait_ge(s["xn_done" if task == "xT" else "xn2"], n + 1)
                    for i in range(TJ):
                        last = nc.tensor.transpose(misc[:, i * P:(i + 1) * P], xn[:, task == "xT2", i, :], ident[:])
                elif task in ("q", "qf", "k", "kf"):
                    last = mm(misc[:], wT[:, ("q", "qf", "k", "kf").index(task), :], xnT[:])
                elif task == "v":
                    for i in range(TJ):
                        last = mm(misc[:, i * P:(i + 1) * P], xnT[:, i * P:(i + 1) * P], wT[:, 4, :])
                elif task == "aT":
                    pe.wait_ge(s["at_done"], NG * (n + 1))
                    for i in range(TJ):
                        last = nc.tensor.transpose(misc[:, i * P:(i + 1) * P], attn[:, i, :], ident[:])
                elif task == "y":
                    for i in range(TJ):
                        last = mm(misc[:, i * P:(i + 1) * P], ot[:, i * P:(i + 1) * P], wT[:, 5, :])
                elif task == "lg":
                    for i in range(TJ):
                        last = mm(misc[:, i * NE:(i + 1) * NE], xfT[:, i * P:(i + 1) * P], rwT[:])
                elif task == "wT":
                    pe.wait_ge(s["r_pool"], 3 * (n + 1))
                    last = nc.tensor.transpose(misc[:, 0:P], wtok[:].rearrange("p t e -> p (t e)"), ident[:])
                last.then_inc(s["misc_pe"], 1)

            pe.wait_ge(s["z_pool"], 2)
            mm(accb[:], zb[:], zr[:])
            def turn(i, buf, slot):
                pe.wait_ge(ew_in[buf], 48 * i + 48)
                for k in range(3):
                    last = nc.tensor.transpose(pair[slot][:, k // 2, (k % 2) * D:(k % 2 + 1) * D], ewn[:, buf, k, :], ident[:])
                last.then_inc(s["et_pe"], 1)

            def gate_up(e, buf, J, slot, used):
                if J == 0:
                    pe.wait_ge(s["eh_act"], 2 * e + 2)
                    pe.wait_ge(s["el_dve"], e + 1)
                for k, free, done in ((0, "ga_dve", "gt_pe"), (1, "hh_dve", "gu_pe")):
                    if used is not None:
                        pe.wait_ge(s[free], used)
                    o = pair[slot][:, k, :]
                    mm(o, ehi[:, buf, k, :], xh[:, tok(J)], stop=False)
                    mm(o, ehi[:, buf, k, :], xl[:, tok(J)], start=False, stop=False)
                    mm(o, elo[:, buf, k, :], xh[:, tok(J)], start=False).then_inc(s[done], 1)

            def zero(J):
                mm(out_bank[J][:], zb[:], zr[:], stop=False, loose=True)

            def down(m, buf, J, k):
                pe.wait_ge(s["hw_pool"], m + 1)
                mm(out_bank[J][:], edn[:, buf, :], hw[:, k, :], start=False, stop=False, loose=True).then_inc(s["dn_pe"], 1)

            def head_down(m):
                e, J = HEAD[m]
                if J == NJ - 1 and e == 0:
                    pe.wait_ge(s["misc_read"], len(USE))
                    zero(J)
                down(m, e % 2, J, m % NJ)

            def head_block(m):
                ahead = m in TURN_AT and m >= 2 and HEAD[m - 2][0] == TURN_AT[m] - 2
                if ahead:
                    head_down(m - 2)
                if m in TURN_AT:
                    slot, (_, used) = SLOTS["turn", TURN_AT[m]]
                    pe.wait_ge(s["hh_dve"], used + 1)
                    turn(TURN_AT[m] // 2, TURN_AT[m] % 2, slot)
                slot, before = SLOTS["block", m]
                e, J = HEAD[m]
                if J == NJ - 1 and e == 0:
                    pe.wait_ge(s["low_done"], NJ)
                if before and before[0] == "turn":
                    pe.wait_ge(s["eh_act"], 2 * before[1] + 2)
                    pe.wait_ge(s["el_dve"], before[1] + 1)
                    if before[1] == 3:
                        pe.wait_ge(s["wt_done"], NJ)
                gate_up(e, e % 2, J, slot, before[1] + 1 if before and before[0] == "block" else None)
                if m >= 2 and not ahead:
                    head_down(m - 2)

            for v in range(FIRST, MOE + len(HEAD)):
                scans = SCAN_AT.get(v, [])
                for part in range(4):
                    for q in scans[part * len(scans) // 4:(part + 1) * len(scans) // 4]:
                        pe_max(q)
                    if part % 2 == 1 and LAG <= v < NSTEP + LAG:
                        pe_av(v - LAG, part // 2)
                    if part % 2 == 0 and 0 <= v < NSTEP:
                        pe_scores(v, part // 2)
                m = v - MOE
                if m == -1:
                    turn(0, 0, SLOTS["turn", 0][0])
                late = m in TURN_AT and TURN_AT[m] == NSH - 1
                if not late:
                    for task, n in tasks("pe", v):
                        pe_task(task, n)
                if m == 0:
                    pe.wait_ge(s["low_done"], NJ - 1)
                    pe.wait_ge(s["mx_rd"], len(SCANS))
                    pe.wait_ge(s["ot_act"], NB)
                    for J in range(NJ - 1):
                        zero(J)
                if m >= 0:
                    head_block(m)
                if late:
                    for task, n in tasks("pe", v):
                        pe_task(task, n)

            with pe.Fori(NSH // 2, NX // 2) as i:
                for k in range(2):
                    e = 2 * i + k
                    n = e * NJ
                    gate_up(e, k, 0, k, None)
                    down(n - 2, 1 - k, NJ - 2, NJ - 2)
                    gate_up(e, k, 1, 1 - k, n)
                    down(n - 1, 1 - k, NJ - 1, NJ - 1)
                    gate_up(e, k, 2, k, n + 1)
                    down(n, k, 0, 0)
                    pe.wait_ge(s["hh_dve"], n + 2)
                    turn(i + k, 1 - k, 1 - k)
                    gate_up(e, k, 3, k, n + 3)
                    down(n + 1, k, 1, 1)
            for J in range(NJ):
                if J >= NJ - 2:
                    down(NX * NJ + J - NJ, 1, J, J)
                mm(out_bank[J][:], zb[:], zr[:], start=False, loose=True).then_inc(s["acc0"], 1)
            pe.wait_ge(s["eh_act"], 2 * (NX + 1))
            pe.wait_ge(s["el_dve"], NX + 1)
            for J in range(NJ):
                pe.wait_ge(s["fin_act"], J + 1)
                for i in range(TJ):
                    last = nc.tensor.transpose(pair[J // 2][:, J % 2, i * P:(i + 1) * P], fin[:, J, i * P:(i + 1) * P], ident[:])
                last.then_inc(s["ft_pe"], 1)

        @block.vector
        def _(dve):
            def behind(J):
                dve.memset(kst[64:P, J].rearrange("p h s -> p (h s)").bitcast(F32), TWO_ONES).then_inc(s["stk_dve"], 1)

            def constants():
                dve.wait_ge(s["rwt_pe"], 1)
                dve.tensor_copy(rwT[:], bank[0][:, 0:NE]).then_inc(s["rwt_dve"], 1)
                dve.wait_ge(s["c_done"], 4)
                dve.tensor_copy(iota_e[:], iota_i[:]).then_inc(s["rwt_dve"], 1)

            def dve_max(q):
                b, i, c, h, m = SCANS[q]
                J, G = GROUPS[b]
                n = (i + 1) * P if c == J else BT
                if b >= 2 and SCANS[q - 1][0] != b:
                    dve.wait_ge(s["mx_fin"], b - 1)
                dve.wait_ge(s["mm_pe"], q + 1)
                dve.tensor_reduce(pmax[:, b % 2, h:h + m, i, c], bank[q % 2][:, 0:m * n].rearrange("p (h k) -> p h k", h=m),
                                  AX, ALU.max).then_inc(s["mx_rd"], 1)

            def last_max(b):
                J, G = GROUPS[b]
                dve.wait_ge(s["mx_rd"], SCANNED[b])
                if b >= 2:
                    dve.wait_ge(s["misc_pe"], USE[("max", b - 2)] + 1)
                dve.tensor_reduce(negm[:, b % 2, :], pmax[:, b % 2, :, :, 0:J + 1].rearrange("p h i c -> p (h i) c"), AX,
                                  ALU.max, negate=True).then_inc(s["mx_fin"], 1)

            rows = misc[:].rearrange("p (i h r) -> p i h r", i=TJ, h=HG)

            def out_sums(b):
                dve.wait_ge(s["misc_pe"], USE[("out", b)] + 1)
                if b:
                    dve.wait_ge(s["at_done"], b)
                dve.reciprocal(rsum[:], rows[:, :, :, DK]).then_inc(s["rs_out"], 1)

            def out_scaled(b):
                J, G = GROUPS[b]
                dve.wait_ge(s["rs_out"], b + 1)
                if J and G == 0:
                    dve.wait_ge(s["misc_pe"], USE[("aT", J - 1)] + 1)
                dst = attn[:].rearrange("p i (g h r) -> p i g h r", g=NG, h=HG)
                dve.tensor_tensor(dst[:, :, G], rows[:, :, :, 0:DK], rsum[:].unsqueeze(3).to_broadcast([P, TJ, HG, DK]),
                                  ALU.mult).then_inc(s["at_done"], 1)
                dve.wait_ge(s["at_done"], b + 1)
                dve.sem_inc(s["misc_read"], 1)

            def statistics(st, which, J):
                for i in range(TJ):
                    last = dve.bn_stats(stats[:, which, i, :], xs[:, J * TJ + i, :])
                last.then_inc(s[st], 1)

            def aggregate(st, ag, done, which, J):
                dve.wait_ge(s[st], J + 1)
                if J:
                    dve.wait_ge(s[done], J)
                for i in range(TJ):
                    dve.bn_aggr(mv[:, which, i, :], stats[:, which, i, :]).then_inc(s[ag], 1)

            def rope_product(task, J):
                side, flip = ("q", "qf", "k", "kf").index(task) // 2, task[1:] == "f"
                table, dst = (sin_t, csin) if flip else (cos_t, ccos)
                if J < 2:
                    k = 2 * side + flip
                    done, n, src = "proj_read", 4 * J + k + 1, pair[side][:, int(flip), :]
                    dve.wait_ge(s["proj_pe"], n)
                else:
                    done, n, src = "misc_read", USE[(task, J)] + 1, misc[:]
                    dve.wait_ge(s["misc_pe"], n)
                if task == "q":
                    dve.wait_ge(tab_in[J], 32)
                if J:
                    dve.wait_ge(s["rp_r1"], 2 * (J - 1) + side + 1)
                    dve.wait_ge(s["rp_p3"], 2 * (J - 1) + side + 1)
                    dve.wait_ge(s["rp_p2"], 2 * (J - 1) + side + 1)
                dve.tensor_tensor(dst[:, side, :], src, table[J == 1], ALU.mult).then_inc(s[done], 1)
                if flip:
                    dve.wait_ge(s[done], n)
                    dve.sem_inc(s["rp_sin"], 1)

            def normalise(rst, done, task, which, J):
                dve.wait_ge(s[rst], J + 1)
                if J:
                    dve.wait_ge(s["misc_pe"], USE[(task, J - 1)] + 1)
                for i in range(TJ):
                    last = dve.tensor_scalar(xn[:, which, i, :], xs[:, J * TJ + i, :], mv[:, which, i, 0:1],
                                             rstd[:, which, i:i + 1], ALU.subtract, ALU.mult)
                last.then_inc(s[done], 1)

            def low(J):
                dve.wait_ge(s["xh_act"], J + 1)
                dve.tensor_tensor(xl[:, tok(J)], xfT[:], xh[:, tok(J)].bitcast(F32), ALU.subtract).then_inc(s["low_done"], 1)

            def rest(J, side):
                dve.wait_ge(s["rp_p1"], 2 * J + side + 1)
                dve.tensor_tensor(csin[:, side, :], ccos[:, side, :], piece[:, side, 0, :], ALU.subtract)\
                    .then_inc(s["rp_r1"], 1)

            def third(J, side):
                dve.wait_ge(s["rp_p2"], 2 * J + side + 1)
                dve.tensor_tensor(piece[:, side, 2, :], csin[:, side, :], piece[:, side, 1, :], ALU.subtract)\
                    .then_inc(s["rp_p3"], 1)

            def residual(J):
                dve.wait_ge(s["misc_pe"], USE[("y", J)] + 1)
                cols = slice(J * TJ, (J + 1) * TJ)
                dve.tensor_tensor(xs[:, cols, :], xs[:, cols, :], misc[:].rearrange("p (i d) -> p i d", i=TJ), ALU.add)\
                    .then_inc(s["misc_read"], 1)

            def route(J, k):
                full, wide = [P, TJ, NE], [P, TJ, TOPK, NE]
                if k == 0:
                    dve.wait_ge(s["misc_pe"], USE[("lg", J)] + 1)
                    dve.wait_ge(s["rw_in"], 32)
                if DVE_ROUTE * J + k:
                    dve.wait_ge(s["r_dve"], DVE_ROUTE * J + k)
                if k == 3:
                    dve.wait_ge(s["r_act"], J + 1)
                if k == 12 and J:
                    dve.wait_ge(s["r_pool"], 3 * J)
                if k == 0:
                    last = dve.tensor_tensor(lg[:], misc[:, 0:TJ * NE].rearrange("p (t e) -> p t e", t=TJ),
                                             bias[:].unsqueeze(1).to_broadcast(full), ALU.add)
                elif k == 1:
                    last = dve.tensor_reduce(mx[:], lg[:], AX, ALU.max)
                elif k == 2:
                    last = dve.tensor_tensor(sc[:], lg[:], mx[:].unsqueeze(2).to_broadcast(full), ALU.subtract)
                elif k == 3:
                    last = dve.tensor_reduce(sm[:], ex[:], AX, ALU.add)
                elif k == 4:
                    last = dve.reciprocal(rs[:], sm[:])
                elif k == 5:
                    last = dve.tensor_tensor(lg[:], ex[:], rs[:].unsqueeze(2).to_broadcast(full), ALU.mult)
                elif k == 6:
                    for t in range(TJ):
                        last = dve.max(top[:, t, :], lg[:, t, :])
                elif k == 7:
                    for t in range(TJ):
                        last = dve.max_index(idx[:, t, :], top[:, t, :], lg[:, t, :])
                elif k == 8:
                    last = dve.tensor_copy(idxf[:], idx[:, :, 0:TOPK])
                elif k == 9:
                    last = dve.tensor_reduce(ts4[:], top[:, :, 0:TOPK], AX, ALU.add)
                elif k == 10:
                    last = dve.tensor_scalar(tc4[:], ts4[:], 1e-12, 2.0, ALU.max, ALU.mult)
                elif k == 11:
                    last = dve.reciprocal(tr4[:], tc4[:])
                elif k == 12:
                    last = dve.tensor_tensor(w4[:], top[:, :, 0:TOPK], tr4[:].unsqueeze(2).to_broadcast([P, TJ, TOPK]), ALU.mult)
                else:
                    last = dve.tensor_tensor(hot[:], iota_e[:].unsqueeze(1).unsqueeze(1).to_broadcast(wide),
                                             idxf[:].unsqueeze(3).to_broadcast(wide), ALU.is_equal)
                last.then_inc(s["r_dve"], 1)
                if k == 0:
                    dve.wait_ge(s["r_dve"], DVE_ROUTE * J + 1)
                    dve.sem_inc(s["misc_read"], 1)

            def dve_task(task, *a):
                if task == "stats":
                    dve.wait_ge(x_in_s[a[0]], 16)
                    if a[0]:
                        dve.wait_ge(s["ag_done"], TJ * a[0])
                    statistics("st_done", 0, *a)
                elif task == "stats2":
                    dve.wait_ge(s["misc_read"], USE[("y", a[0])] + 1)
                    statistics("st2", 1, *a)
                elif task == "aggr":
                    aggregate("st_done", "ag_done", "xn_done", 0, *a)
                elif task == "aggr2":
                    aggregate("st2", "ag2", "xn2", 1, *a)
                elif task == "norm":
                    normalise("rstd_done", "xn_done", "xT", 0, *a)
                elif task == "norm2":
                    normalise("rstd2", "xn2", "xT2", 1, *a)
                elif task in ("q", "qf", "k", "kf"):
                    rope_product(task, *a)
                else:
                    {"low": low, "r1": rest, "p3": third, "sums": out_sums, "out": out_scaled, "y": residual, "route": route}[task](*a)

            def low_parts(e, buf, slot):
                dve.wait_ge(s["eh_act"], 2 * e + 1)
                dve.tensor_tensor(elo[:, buf, :, :].rearrange("p a d -> p (a d)"), pair[slot][:, 0, 0:2 * D],
                                  ehi[:, buf, :, :].rearrange("p a d -> p (a d)").bitcast(F32), ALU.subtract)\
                    .then_inc(s["el_dve"], 1)

            def hidden(m, par, slot):
                later = not isinstance(m, int) or m >= 2
                dve.wait_ge(s["th_act"], m + 1)
                if later:
                    dve.wait_ge(s["hh_dve"], m - 1)
                dve.scalar_tensor_tensor(ga[:, par, :], th[:, par, :], 1.0, pair[slot][:, 0, :], ALU.add, ALU.mult)\
                    .then_inc(s["ga_dve"], 1)
                dve.wait_ge(s["ga_dve"], m + 1)
                dve.wait_ge(s["gu_pe"], m + 1)
                if later:
                    dve.wait_ge(s["hw_pool"], m - 1)
                dve.tensor_tensor(hh[:, par, :], ga[:, par, :], pair[slot][:, 1, :], ALU.mult).then_inc(s["hh_dve"], 1)

            behind(0)
            for v in range(FIRST, MOE + len(HEAD)):
                if v == FIRST + 1:
                    constants()
                elif v == FIRST + 3:
                    behind(1)
                small = tasks("dve", v)
                m = v - MOE
                if m == -1:
                    low_parts(0, 0, SLOTS["turn", 0][0])
                if m in TURN_AT:
                    e = TURN_AT[m]
                    low_parts(e, e % 2, SLOTS["turn", e][0])
                for q in SCAN_AT.get(v, []):
                    dve_max(q)
                    if q + 1 in SCANNED:
                        last_max(SCANNED.index(q + 1))
                    for task in small[:1]:
                        dve_task(*task)
                    small = small[1:]
                for task in small:
                    dve_task(*task)
                if m >= 0:
                    hidden(m, m % 2, SLOTS["block", m][0])

            with dve.Fori(NSH // 2, NX // 2) as i:
                for k in range(2):
                    e = 2 * i
                    n = (e + k) * NJ
                    hidden(n, 0, k)
                    hidden(n + 1, 1, 1 - k)
                    hidden(n + 2, 0, k)
                    low_parts(e + (k + 1), 1 - k, 1 - k)
                    hidden(n + 3, 1, k)
            for J in range(NJ):
                cols = slice(J * TJ, (J + 1) * TJ)
                dve.wait_ge(s["ft_pe"], J + 1)
                dve.tensor_tensor(yo[:, cols, :], xs[:, cols, :],
                                  pair[J // 2][:, J % 2, :].rearrange("p (i d) -> p i d", i=TJ), ALU.add)\
                    .then_inc(s["yo_dve"], 1)


_INS = ["L0_attn_x", "L0_attn_W_Q", "L0_attn_W_K", "L0_attn_W_V", "L0_attn_W_O", "L0_ffn_router_w",
        "L0_ffn_router_bias", "L0_ffn_gate_w", "L0_ffn_up_w", "L0_ffn_down_w", "L0_ffn_sgate_w", "L0_ffn_sup_w",
        "L0_ffn_sdown_w"]


def rope_tables():
    theta = np.float32(1.0) / np.float32(10000.0) ** (np.arange(0, DK, 2, dtype=np.float32) / np.float32(DK))
    ang = np.outer(np.arange(S, dtype=np.float32), theta.astype(np.float32)).astype(np.float32)
    ang = np.concatenate([ang, ang], axis=1).T
    sign = np.where(np.arange(DK) < DK // 2, -1.0, 1.0).astype(np.float32)[:, None]
    cos, sin = np.cos(ang).astype(np.float32), (np.sin(ang).astype(np.float32) * sign).astype(np.float32)
    return np.repeat(cos, NH, axis=0), np.repeat(sin, NH, axis=0)


def kernel(**inputs):
    import concourse.bacc as _bacc
    from concourse.bass_utils import run_bass_kernel_spmd as _run

    nc = _bacc.Bacc("TRN2", target_bir_lowering=False, num_devices=1)
    arrays, args = {}, []
    cos, sin = rope_tables()
    for name, a in [(n, inputs[n]) for n in _INS] + [("rope_cos", cos), ("rope_sin", sin)]:
        a = np.ascontiguousarray(a)
        arrays[f"in_{name}"] = a
        args.append(nc.dram_tensor(f"in_{name}", a.shape, mybir.dt.from_np(a.dtype), kind="ExternalInput").ap())
    args.append(nc.dram_tensor("out_0", (1, S, D), F32, kind="ExternalOutput").ap())
    mixer(nc, *args)
    r = _run(nc, [arrays], core_ids=[0])
    return r.results[0]["out_0"]
```
